# Optimizing a Trainium2 kernel written in Bass

```python
import numpy as np
import jax
import jax.numpy as jnp

def _softmax(x, axis=-1):
    return jax.nn.softmax(x, axis=axis)

def _gelu(x):
    return jax.nn.gelu(x, approximate=True)

def _silu(x):
    return jax.nn.silu(x)

def _sigmoid(x):
    return jax.nn.sigmoid(x)

def _layernorm(x, axis=-1, eps=1e-05):
    m = jnp.mean(x, axis=axis, keepdims=True)
    v = jnp.var(x, axis=axis, keepdims=True)
    return (x - m) / jnp.sqrt(v + eps)

def _scatter_add(tgt, idx, src, axis=0):
    return tgt.at[idx].add(src)

def _segment_sum(src, seg, n):
    return jax.ops.segment_sum(src, seg, n)
kernel_name = 'mk_decoder_postln_d1_seqx_r8_3b9038'

def setup_inputs(seed: int=0):
    np.random.seed(seed)
    _w = jnp.asarray

    def _rec_inputs():
        import jax
        import jax.numpy as jnp
        _rk = jax.random.key(seed)
        x = -0.000125 + 0.9999 * jax.random.normal(jax.random.fold_in(_rk, 1), (4, 256, 256), jnp.float32)
        _lenS = 256 - jax.random.randint(jax.random.fold_in(_rk, 7), (4,), 0, max(1, 256 // 4) + 1, jnp.int32)
        _lenS2 = 256 - jax.random.randint(jax.random.fold_in(_rk, 8), (4,), 0, max(1, 256 // 4) + 1, jnp.int32)
        itok_BxS_13_99985 = jax.random.randint(jax.random.fold_in(_rk, 11), (4, 256), 13, 99986, jnp.int32)
        _ctx_2048P = jax.random.normal(jax.random.fold_in(_rk, 12), (4, 16, 256), jnp.float32)
        _ctx_2048c = jax.random.dirichlet(jax.random.fold_in(_rk, 512), 0.3 * jnp.ones((16,), jnp.float32), (4, 256))
        _ctx_2048t = jnp.einsum('bsk,bkd->bsd', _ctx_2048c, _ctx_2048P)
        _ctx_2048t = _ctx_2048t * jax.lax.rsqrt(jnp.mean(jnp.square(_ctx_2048t)) + 1e-12) * 0.953939
        ctx_2048 = 6.82029e-06 + 0.0200006 * (_ctx_2048t + 0.3 * jax.random.normal(jax.random.fold_in(_rk, 612), (4, 256, 256), jnp.float32))
        return (x, itok_BxS_13_99985, ctx_2048)
    x, itok_BxS_13_99985, ctx_2048 = _rec_inputs()

    def _L0_attn_setup():
        import jax, jax.numpy as jnp
        import numpy as np
        HIDDEN = 256
        NUM_HEADS = 16
        HEAD_DIM = HIDDEN // NUM_HEADS
        RANK = 64
        BATCH = 1
        SEQ = 256
        key = jax.random.key(seed)
        k1, k2, k3, k4, k5 = jax.random.split(key, 5)
        s_in = 0.02
        return {'hidden_states': jax.random.normal(k1, (BATCH, SEQ, HIDDEN), jnp.float32), 'Wq': jax.random.normal(k2, (RANK, HIDDEN), jnp.float32) * s_in, 'Wk': jax.random.normal(k3, (RANK, HIDDEN), jnp.float32) * s_in, 'Wv': jax.random.normal(k4, (HIDDEN, HIDDEN), jnp.float32) * s_in, 'Wo': jax.random.normal(k5, (HIDDEN, HIDDEN), jnp.float32) * s_in}
    _L0_attn_all = _L0_attn_setup()
    _L0_attn_in = {k: v for k, v in _L0_attn_all.items() if k in ('Wq', 'Wk', 'Wv', 'Wo')}
    del _L0_attn_all

    def _L0_xattn_setup():
        import jax, jax.numpy as jnp
        import numpy as np
        B, S, D = (4, 512, 256)
        E = 4
        F = 1024 // E
        VOCAB = 12500
        key = jax.random.key(seed)
        k1, k2, k3, k4, k5 = jax.random.split(key, 5)
        hidden_states = jax.random.normal(k1, (B, S, D), dtype=jnp.float32)
        token_ids = jax.random.randint(k2, (B, S), 0, VOCAB, dtype=jnp.int64)
        Wg = jax.random.normal(k3, (E, F, D), dtype=jnp.float32) * 0.02
        Wu = jax.random.normal(k4, (E, F, D), dtype=jnp.float32) * 0.02
        Wd = jax.random.normal(k5, (E, D, F), dtype=jnp.float32) * 0.02
        return {'hidden_states': hidden_states, 'token_ids': token_ids, 'Wg': Wg, 'Wu': Wu, 'Wd': Wd}
    _L0_xattn_all = _L0_xattn_setup()
    _L0_xattn_in = {k: v for k, v in _L0_xattn_all.items() if k in ()}
    del _L0_xattn_all

    def _L0_ffn_setup():
        import jax, jax.numpy as jnp
        import numpy as np
        D_MODEL = 256
        D_FF = 1024
        N_EXPERTS = 4
        B, S = (2, 256)
        key = jax.random.key(seed)
        ks = jax.random.split(key, 6)
        scale = 0.02
        return {'hidden_states': jax.random.normal(ks[0], (B, S, D_MODEL), dtype=jnp.float32), 'Wr': jax.random.normal(ks[1], (D_MODEL, N_EXPERTS), dtype=jnp.float32) * scale, 'br': jnp.zeros((N_EXPERTS,), dtype=jnp.float32), 'Wg': jax.random.normal(ks[2], (N_EXPERTS, D_MODEL, D_FF), dtype=jnp.float32) * scale, 'Wu': jax.random.normal(ks[3], (N_EXPERTS, D_MODEL, D_FF), dtype=jnp.float32) * scale, 'Wd': jax.random.normal(ks[4], (N_EXPERTS, D_FF, D_MODEL), dtype=jnp.float32) * scale}
    _L0_ffn_all = _L0_ffn_setup()
    _L0_ffn_in = {k: v for k, v in _L0_ffn_all.items() if k in ('Wr', 'br', 'Wg', 'Wu', 'Wd')}
    del _L0_ffn_all
    return {'x': x, 'itok_BxS_13_99985': itok_BxS_13_99985, 'ctx_2048': ctx_2048, 'L0_attn_Wq': _L0_attn_in['Wq'], 'L0_attn_Wk': _L0_attn_in['Wk'], 'L0_attn_Wv': _L0_attn_in['Wv'], 'L0_attn_Wo': _L0_attn_in['Wo'], 'L0_ffn_Wr': _L0_ffn_in['Wr'], 'L0_ffn_br': _L0_ffn_in['br'], 'L0_ffn_Wg': _L0_ffn_in['Wg'], 'L0_ffn_Wu': _L0_ffn_in['Wu'], 'L0_ffn_Wd': _L0_ffn_in['Wd']}

def reference(x, itok_BxS_13_99985, ctx_2048, L0_attn_Wq, L0_attn_Wk, L0_attn_Wv, L0_attn_Wo, L0_ffn_Wr, L0_ffn_br, L0_ffn_Wg, L0_ffn_Wu, L0_ffn_Wd):
    import jax
    import jax.numpy as jnp

    def _L0_attn_ref(hidden_states, Wq, Wk, Wv, Wo):
        import jax, jax.numpy as jnp
        import numpy as np
        HIDDEN = 256
        NUM_HEADS = 16
        HEAD_DIM = HIDDEN // NUM_HEADS
        RANK = 64
        BATCH = 1
        SEQ = 256
        b, s, _ = hidden_states.shape
        qf = hidden_states @ Wq.T
        kf = hidden_states @ Wk.T
        head_f = jnp.ones((NUM_HEADS, RANK), hidden_states.dtype)
        scores = jnp.einsum('hr,bir,bjr->bhij', head_f, qf, kf)
        attn = jax.nn.softmax(scores.astype(jnp.float32), axis=-1).astype(hidden_states.dtype)
        v = (hidden_states @ Wv.T).reshape(b, s, NUM_HEADS, HEAD_DIM).transpose(0, 2, 1, 3)
        out = jnp.einsum('bhij,bhjd->bhid', attn, v)
        out = out.transpose(0, 2, 1, 3).reshape(b, s, HIDDEN)
        return out @ Wo.T

    def _L0_xattn_ref(hidden_states, token_ids, Wg, Wu, Wd):
        import jax, jax.numpy as jnp
        import numpy as np
        B, S, D = (4, 512, 256)
        E = 4
        F = 1024 // E
        VOCAB = 12500
        tokens_per_expert = VOCAB // E
        tid = jnp.clip(token_ids, 0, VOCAB - 1)
        expert_ids = jnp.minimum(tid // tokens_per_expert, E - 1)
        out = jnp.zeros_like(hidden_states)
        for e in range(E):
            g = jax.nn.silu(jnp.einsum('bsd,fd->bsf', hidden_states, Wg[e]))
            u = jnp.einsum('bsd,fd->bsf', hidden_states, Wu[e])
            y = jnp.einsum('bsf,df->bsd', g * u, Wd[e])
            out = jnp.where((expert_ids == e)[..., None], y, out)
        return out

    def _L0_ffn_ref(hidden_states, Wr, br, Wg, Wu, Wd):
        import jax, jax.numpy as jnp
        import numpy as np
        D_MODEL = 256
        D_FF = 1024
        N_EXPERTS = 4
        B, S = (2, 256)
        b, s, d = hidden_states.shape
        x = hidden_states.reshape(-1, d)
        logits = x @ Wr + br
        probs = jax.nn.softmax(logits, axis=-1)
        top_w, top_idx = jax.lax.top_k(probs, 1)
        g = jnp.einsum('td,edf->tef', x, Wg)
        u = jnp.einsum('td,edf->tef', x, Wu)
        h = jax.nn.silu(g) * u
        y = jnp.einsum('tef,efd->ted', h, Wd)
        sel = jnp.take_along_axis(y, top_idx[:, :, None], axis=1)[:, 0]
        out = sel * top_w
        return out.reshape(b, s, d)
    x = _layernorm(x + _L0_attn_ref(x, L0_attn_Wq, L0_attn_Wk, L0_attn_Wv, L0_attn_Wo), axis=-1)
    x = _layernorm(x + _L0_xattn_ref(x, itok_BxS_13_99985, ctx_2048, ctx_2048, ctx_2048), axis=-1)
    x = _layernorm(x + _L0_ffn_ref(x, L0_ffn_Wr, L0_ffn_br, L0_ffn_Wg, L0_ffn_Wu, L0_ffn_Wd), axis=-1)
    return x

_drawn_inputs = setup_inputs


def setup_inputs(seed=0):
    import zlib

    import numpy as np

    out = dict(_drawn_inputs(seed))
    spreads = {'L0_ffn_br': (0.0, 0.8)}
    factors = {'L0_attn_Wq': 6.098,
     'L0_attn_Wk': 5.497,
     'L0_attn_Wv': 4.701,
     'L0_attn_Wo': 4.74,
     'L0_ffn_Wr': 5.688,
     'L0_ffn_Wg': 4.804,
     'L0_ffn_Wu': 4.728,
     'L0_ffn_Wd': 4.749}
    for name, (base, spread) in spreads.items():
        noise = np.random.default_rng([zlib.crc32(name.encode()), seed]).standard_normal(out[name].shape)
        drawn = base * np.exp(spread * noise) if base else spread * noise
        out[name] = jnp.asarray(drawn.astype(out[name].dtype))
    for name, factor in factors.items():
        out[name] = (out[name] * factor).astype(out[name].dtype)
    return out
```

```python
from contextlib import ExitStack

import numpy as np
import concourse.bass as bass
from concourse import mybir

ALU = mybir.AluOpType
ACT = mybir.ActivationFunctionType
AX = mybir.AxisListType
F32 = mybir.dt.float32
F32R = mybir.dt.float32r
BF16 = mybir.dt.bfloat16
I32 = mybir.dt.int32

P = 128
D = 256
DK = D // P
BATCH, SEQ = 4, 256
TOKENS = BATCH * SEQ
CHUNKS = TOKENS // P
RANK = 64
E = 4
VOCAB = 12500
PER_EXPERT = VOCAB // E
F = 1024
NQ = 4
FQ = F // NQ
T = (TOKENS + E * (P - 1)) // P
EPS = 1e-5
FAR = float(1 << 20)

TOK, LOG, ROW = D, D + 1, 264
QKW = DK * 2 * RANK
REGION = TOKENS
BLOCKS2 = (E - 1) * (REGION // P) + T
RING = 6
PIECE = 512
GU = DK * 2 * FQ
CHUNK = GU + (FQ // P) * D
SLOTS = 3
CTX_CHUNK = (E // 2) * DK * D
N_CTX = 2


def route_kernel(nc, aw, xT_in, x_in, ids_in, wr_in, br_in, ctx_in, wffn_in, out):
    scr1 = nc.dram_tensor("x1_sorted", (T * P, ROW), F32).ap()
    scr2 = nc.dram_tensor("x2_sorted", (BLOCKS2 * P, ROW), F32).ap()

    with ExitStack() as ctx:
        def sb(name, shape, dt=F32):
            return ctx.enter_context(nc.sbuf_tensor(name, shape, dt))

        def sem(name):
            return ctx.enter_context(nc.semaphore(name))

        w_hi = sb("w_hi", [P, 2 * E * CHUNK], F32R)
        w_lo = sb("w_lo", [P, 2 * E * CHUNK], F32R)
        xr = sb("xr", [P, T * 2 * D], F32R)
        hT = sb("hT", [P, 2, 2, FQ], F32R)
        stage = sb("stage", [P, SLOTS, CHUNK])
        arena = sb("arena", [P, 9984])
        rows = sb("rows", [P, T, ROW])
        ring = sb("ring", [P, RING, ROW])
        gate = sb("gate", [P, 2, FQ])
        hid = sb("hid", [P, 2, FQ])
        x2T = sb("x2T", [P, D])
        padrow = sb("padrow", [P, ROW])
        ident = sb("ident", [P, P])
        below = sb("below", [P, P], BF16)
        ones = sb("ones", [P, P], BF16)
        ids = sb("ids", [P, CHUNKS], I32)
        wr = sb("wr", [P, DK, E])
        br = sb("br", [1, E])
        one_row = sb("one_row", [1, P])
        tok = sb("tok", [P, CHUNKS])
        tile_no = sb("tile_no", [P, T])
        fill = sb("fill", [P, E, CHUNKS])
        prio = sb("prio", [P, E])
        base2 = sb("base2", [P, E])
        mhalf = sb("mhalf", [P, 2])
        idf = sb("idf", [P, CHUNKS])
        ge1 = sb("ge1", [P, E + 1, CHUNKS])
        m1 = sb("m1", [P, CHUNKS, E], BF16)
        m1cum = sb("m1cum", [P, CHUNKS + 1, E], BF16)
        pos1 = sb("pos1", [P, CHUNKS, E])
        slot1f = sb("slot1f", [P, CHUNKS])
        slot1 = sb("slot1", [P, CHUNKS], I32)
        m2 = sb("m2", [P, T, E], BF16)
        m2cum = sb("m2cum", [P, T + 1, E], BF16)
        pos2 = sb("pos2", [P, 2, E])
        slot2f = sb("slot2f", [P, T])
        slot2 = sb("slot2", [P, T], I32)
        valid = sb("valid", [P, T])
        far = sb("far", [P, T])
        gt = sb("gt", [P, E, CHUNKS])
        ntile = sb("ntile", [P, E])
        first = sb("first", [P, E])
        first128 = sb("first128", [P, E])
        past = sb("past", [P, T, E])
        pastf = sb("pastf", [P, T, E])
        expert = sb("expert", [P, T])
        begun = sb("begun", [P, T])
        blk = sb("blk", [P, T])
        off1 = sb("off1", [P, T], I32)
        off2 = sb("off2", [P, T], I32)
        row2 = sb("row2", [P, T], I32)
        outidx = sb("outidx", [P, T], I32)
        negmax = sb("negmax", [P, 2, 2])
        esum = sb("esum", [P, 2, 2])
        rinv = sb("rinv", [P, 2, 2])
        stats = sb("stats", [P, 2, 6])
        mv = sb("mv", [P, 2, 2, 2])
        rstd = sb("rstd", [P, 2, 2])
        lmax = sb("lmax", [P, 1])
        lw = sb("lw", [P, E])
        lwmax = sb("lwmax", [P, 1])
        lexp = sb("lexp", [P, T, E])
        lsum = sb("lsum", [P, T])
        topw = sb("topw", [P, T])

        cut = [0]

        def carve(n):
            cut[0] += n
            return arena[:, cut[0] - n:cut[0]]

        xT = carve(DK * TOKENS).rearrange("p (k n) -> p k n", k=DK)
        xn = carve(CHUNKS * D).rearrange("p (c d) -> p c d", c=CHUNKS)
        awt = carve(DK * (2 * RANK + 2 * D))
        wqk = awt[:, 0:DK * 2 * RANK].rearrange("p (k n) -> p k n", k=DK)
        wv = awt[:, 256:256 + DK * D].rearrange("p (k n) -> p k n", k=DK)
        woT = awt[:, 768:768 + DK * D].rearrange("p (k n) -> p k n", k=DK)
        wvo = carve(DK * D).rearrange("p (k n) -> p k n", k=DK)
        zt = carve(2 * 2 * D).rearrange("p (b c d) -> p b c d", b=2, c=2)
        at = carve(2 * 2 * SEQ).rearrange("p (b i j) -> p b i j", b=2, i=2)
        aT = carve(2 * 2 * SEQ).rearrange("p (b j i) -> p b j i", b=2, j=2)
        qk = carve(2 * 2 * SEQ).rearrange("p (b w i) -> p b w i", b=2, w=2)[0:RANK]
        acc = arena[:, 0:T * D].rearrange("p (t d) -> p t d", t=T)

        ctx_hi, ctx_lo = xr[:, 0:E * DK * D], xr[:, E * DK * D:2 * E * DK * D]
        X1T = 2 * E * DK * D

        def x1T(t, part):
            o = X1T + (t % 2) * 2 * D + part * D
            return xr[:, o:o + D]

        def x2s(t, part):
            o = t * 2 * D + part * D
            return xr[:, o:o + D]

        bank = [ctx.enter_context(nc.psum_tensor(f"bank{i}", [P, 512], F32)) for i in range(8)]
        pQK, pZ, pS, pT, pO, pR1, pW = bank[0], bank[1], bank[2:4], bank[4], bank[5], bank[6], bank[7]
        pX, pG, pH, pY, pC, pL, pR = bank[0], bank[1], bank[2], bank[3], bank[4], bank[5], bank[6]
        fX = [bank[0], bank[7]]
        fA, fH, fY = [bank[1], bank[5]], [bank[2], bank[6]], [bank[3], bank[4]]

        d_aqk, d_avo, d_xT0, d_xT, d_x, d_ids, d_wr = (
            sem(n) for n in ("d_aqk", "d_avo", "d_xT0", "d_xT", "d_x", "d_ids", "d_wr"))
        d_init1, d_init2 = sem("d_init1"), sem("d_init2")
        d_chunk = [sem(f"d_chunk{i}") for i in range(SLOTS)]
        d_rows = [sem(f"d_rows{t}") for t in range(T)]
        d_scat = [sem(f"d_scat{i}") for i in range(RING)]
        consts = sem("consts")
        pad_ready = sem("pad_ready")
        wvo_done, wvo_copied = sem("wvo_done"), sem("wvo_copied")
        m1_ready, r1_done, route1 = sem("m1_ready"), sem("r1_done"), sem("route1")
        qk_done, z_done, s_done, t_done, o_done = (sem(n) for n in ("qk_done", "z_done", "s_done", "t_done", "o_done"))
        qk_copied, z_copied, exp_done, aT_copied = (sem(n) for n in ("qk_copied", "z_copied", "exp_done", "aT_copied"))
        negmax_ready, o_read = sem("negmax_ready"), sem("o_read")
        var_ready, rstd_ready, row_ready = sem("var_ready"), sem("rstd_ready"), sem("row_ready")
        split_hi, split_lo = sem("split_hi"), sem("split_lo")
        dve_step = sem("dve_step")
        x_done, xhi_done, xlo_done, g_done = (sem(n) for n in ("x_done", "xhi_done", "xlo_done", "g_done"))
        silu_done, h_done, ht_done, hhi_done, hlo_done = (
            sem(n) for n in ("silu_done", "h_done", "ht_done", "hhi_done", "hlo_done"))
        y_done, y_read = sem("y_done"), sem("y_read")
        x2_ready, c_done, c_copied = sem("x2_ready"), sem("c_done"), sem("c_copied")
        l_done, mask_ready, r_done, slot_ready = (sem(n) for n in ("l_done", "mask_ready", "r_done", "slot_ready"))
        n_done, tables = sem("n_done"), sem("tables")
        lexp_done, topw_ready = sem("lexp_done"), sem("topw_ready")
        out_ready = sem("out_ready")

        LN1, LN2, LN3 = 0, BATCH, BATCH + T

        def scat(n):
            return d_scat[n % RING], 16 * (n // RING + 1)

        def pieces(n):
            return CTX_CHUNK // PIECE if n < N_CTX else CHUNK // PIECE

        def pieces_to(n):
            return sum(pieces(i) for i in range(n))

        def chunk_of(q, e):
            return N_CTX + q * E + e

        def piece_list(n):
            got = []
            for i in range(pieces(n)):
                src = stage[:, n % SLOTS, i * PIECE:(i + 1) * PIECE]
                if n < N_CTX:
                    o = n * CTX_CHUNK + i * PIECE
                    got.append((src, ctx_hi[:, o:o + PIECE], ctx_lo[:, o:o + PIECE]))
                else:
                    q, e = divmod(n - N_CTX, E)
                    o = ((q % 2) * E + e) * CHUNK + i * PIECE
                    got.append((src, w_hi[:, o:o + PIECE], w_lo[:, o:o + PIECE]))
            return got

        all_pieces = [(n, i) + p for n in range(N_CTX + NQ * E) for i, p in enumerate(piece_list(n))]
        CTX_PIECES = pieces_to(N_CTX)
        Q_PIECES = E * pieces(N_CTX)
        share = [0, 0, 1, 2, 1, 2, 1, 2, 1, 2, 0]
        assert sum(share) == Q_PIECES and len(share) == T

        def quarter_pieces(q, t):
            a = CTX_PIECES + q * Q_PIECES + sum(share[:t])
            return range(a, a + share[t])

        items = [(q, t) for q in range(NQ) for t in range(T)]
        block = ctx.enter_context(nc.Block())

        @block.sync
        def _(sp):
            xT_rows = xT_in.rearrange("p (k n) -> p k n", k=DK)
            sp.dma_start(awt[:, 0:QKW], aw[:, 0:QKW]).then_inc(d_aqk, 16)
            sp.dma_start(xT[:, :, 0:SEQ], xT_rows[:, :, 0:SEQ]).then_inc(d_xT0, 16)
            sp.dma_start(awt[:, QKW:], aw[:, QKW:]).then_inc(d_avo, 16)
            sp.dma_start(xT[:, :, SEQ:], xT_rows[:, :, SEQ:]).then_inc(d_xT, 16)
            sp.wait_ge(pad_ready, 1)
            sp.dma_start(scr1.rearrange("(p r) c -> p r c", p=P),
                         padrow[:].unsqueeze(1).broadcast_to([P, T, ROW])).then_inc(d_init1, 16)
            sp.dma_start(xn, x_in.rearrange("p (c d) -> p c d", c=CHUNKS)).then_inc(d_x, 16)

            def load_chunk(n):
                if n >= SLOTS:
                    sp.wait_ge(split_lo, pieces_to(n - SLOTS + 1))
                src = ctx_in[:, n * CTX_CHUNK:(n + 1) * CTX_CHUNK] if n < N_CTX else wffn_in[n - N_CTX]
                sp.dma_start(stage[:, n % SLOTS, 0:pieces(n) * PIECE], src).then_inc(d_chunk[n % SLOTS], 16)

            for n in range(N_CTX + 2):
                load_chunk(n)
            sp.dma_start(wr[:], wr_in.rearrange("p (k n) -> p k n", k=DK)).then_inc(d_wr, 16)
            sp.dma_start(br[:], br_in).then_inc(d_wr, 16)
            sp.dma_start(scr2.rearrange("(p r) c -> p r c", p=P),
                         padrow[:].unsqueeze(1).broadcast_to([P, BLOCKS2, ROW])).then_inc(d_init2, 16)
            load_chunk(N_CTX + 2)
            for n in range(CHUNKS):
                sp.wait_ge(*scat(n))
            for t in range(T):
                sp.dma_start(rows[:, t, :], scr1[t * P:(t + 1) * P, :]).then_inc(d_rows[t], 16)
            load_chunk(N_CTX + 3)
            for n in range(N_CTX + 4, N_CTX + 7):
                load_chunk(n)
            for n in range(CHUNKS, CHUNKS + T):
                sp.wait_ge(*scat(n))
            sp.wait_ge(tables, 2)
            for t in range(T):
                r = sp.value_load(row2[0:1, t:t + 1], min_val=0, max_val=(BLOCKS2 - 1) * P)
                sp.dma_start(rows[:, t, :], scr2[bass.ds(r, P), :]).then_inc(d_rows[t], 16)
            for n in range(N_CTX + 7, N_CTX + NQ * E):
                load_chunk(n)
            for n in range(CHUNKS + T, CHUNKS + 2 * T):
                sp.wait_ge(*scat(n))

        @block.gpsimd
        def _(pool):
            def const(ins):
                ins.then_inc(consts, 1)
                const.n += 1
            const.n = 0
            g = nc.gpsimd
            const(g.memset(padrow[:], 0.0))
            const(g.memset(ident[:], 1.0))
            const(g.memset(below[:], 1.0))
            const(g.memset(ones[:], 1.0))
            const(g.memset(one_row[:], 1.0))
            const(g.memset(mhalf[:], -0.5))
            const(g.iota(tok[:], pattern=[[P, CHUNKS]], base=0, channel_multiplier=1,
                         allow_small_or_imprecise_dtypes=True))
            const(g.iota(tile_no[:], pattern=[[1, T]], base=0, channel_multiplier=0,
                         allow_small_or_imprecise_dtypes=True))
            const(g.iota(fill[:], pattern=[[0, E], [P, CHUNKS]], base=0, channel_multiplier=0,
                         allow_small_or_imprecise_dtypes=True))
            const(g.iota(prio[:], pattern=[[-1, E]], base=E, channel_multiplier=0,
                         allow_small_or_imprecise_dtypes=True))
            const(g.iota(base2[:], pattern=[[REGION, E]], base=0, channel_multiplier=0,
                         allow_small_or_imprecise_dtypes=True))
            pool.wait_ge(consts, const.n)
            g.memset(padrow[:, TOK:TOK + 1], FAR).then_inc(pad_ready, 1)
            const(g.affine_select(out=ident[:], in_=ident[:], compare_op=ALU.is_equal, fill=0.0, base=0,
                                  pattern=[[-1, P]], channel_multiplier=1))
            const(g.affine_select(out=below[:], in_=below[:], compare_op=ALU.is_gt, fill=0.0, base=0,
                                  pattern=[[1, P]], channel_multiplier=-1))

            def split(k):
                _, _, src, hi, lo = all_pieces[k]
                pool.wait_ge(split_hi, k + 1)
                g.tensor_tensor(out=lo, in0=src, in1=hi.bitcast(F32), op=ALU.subtract).then_inc(split_lo, 1)

            def root(n, buf, width):
                pool.wait_ge(var_ready, n + 1)
                g.tensor_tensor(out=rstd[:, buf, 0:width], in0=mv[:, buf, 0:width, 1], in1=mhalf[:, 0:width],
                                op=ALU.pow).then_inc(rstd_ready, 1)

            pool.wait_ge(route1, 1)
            pool.wait_ge(d_init1, 16)
            done = 0
            for b in range(BATCH):
                root(LN1 + b, b % 2, 2)
                for i in range(2):
                    c = 2 * b + i
                    pool.wait_ge(row_ready, c + 1)
                    g.indirect_dma_start(out=scr1, out_offset=bass.IndirectOffsetOnAxis(ap=slot1[:, c:c + 1], axis=0),
                                         in_=ring[:, c % RING, :], in_offset=None, bounds_check=T * P - 1,
                                         oob_is_err=False).then_inc(d_scat[c % RING], 16)
                split(done)
                done += 1
            pool.wait_ge(d_init2, 16)
            for i in range(T + 4):
                if 1 <= i <= T:
                    root(LN2 + i - 1, (i - 1) % 2, 1)
                if 4 <= i:
                    t = i - 4
                    n = CHUNKS + t
                    pool.wait_ge(slot_ready, t + 1)
                    g.indirect_dma_start(out=scr2, out_offset=bass.IndirectOffsetOnAxis(ap=slot2[:, t:t + 1], axis=0),
                                         in_=ring[:, n % RING, :], in_offset=None, bounds_check=E * REGION - 1,
                                         oob_is_err=False).then_inc(d_scat[n % RING], 16)
                if done < CTX_PIECES + Q_PIECES:
                    split(done)
                    done += 1
            assert done == CTX_PIECES + Q_PIECES
            for q in range(NQ):
                for t in range(T):
                    if q < NQ - 1:
                        for k in quarter_pieces(q + 1, t):
                            split(k)
            for t in range(T):
                n = CHUNKS + T + t
                root(LN3 + t, t % 2, 1)
                pool.wait_ge(out_ready, t + 1)
                g.indirect_dma_start(out=out, out_offset=bass.IndirectOffsetOnAxis(ap=outidx[:, t:t + 1], axis=0),
                                     in_=ring[:, n % RING, 0:D], in_offset=None, bounds_check=TOKENS - 1,
                                     oob_is_err=False).then_inc(d_scat[n % RING], 16)

        @block.tensor
        def _(pe):
            mm, tr = nc.tensor.matmul, nc.tensor.transpose

            def split_mm(dst, xhi, xlo, whi, wlo, start, stop):
                mm(dst, xhi, whi, start=start, stop=False)
                mm(dst, xhi, wlo, start=False, stop=False)
                return mm(dst, xlo, whi, start=False, stop=stop)

            def qk_of(b):
                if b >= 1:
                    pe.wait_ge(qk_copied, 2 * b)
                for k in range(DK):
                    last = mm(pQK[:, 0:SEQ], wqk[:, k, :], xT[:, k, b * SEQ:(b + 1) * SEQ],
                              start=k == 0, stop=k == DK - 1)
                last.then_inc(qk_done, 1)

            pe.wait_ge(d_aqk, 16)
            pe.wait_ge(d_xT0, 16)
            qk_of(0)
            pe.wait_ge(d_avo, 16)
            for d in range(DK):
                for k in range(DK):
                    last = mm(pW[:, d * D:(d + 1) * D], wv[:, k, d * P:(d + 1) * P], woT[:, k, :],
                              start=k == 0, stop=k == DK - 1)
            last.then_inc(wvo_done, 1)
            pe.wait_ge(consts, 13)
            pe.wait_ge(m1_ready, CHUNKS)
            R1 = pR1[:, 0:CHUNKS * E]
            mm(R1, below[:], m1[:].rearrange("p c e -> p (c e)"), start=True, stop=False)
            mm(R1, ones[:], m1cum[:, 0:CHUNKS, :].rearrange("p c e -> p (c e)"), start=False, stop=True)
            mm(pR1[:, 64:64 + E], ones[:], m1cum[:, CHUNKS, :], start=True, stop=True).then_inc(r1_done, 1)

            def front(b):
                if b >= 1:
                    qk_of(b)
                pe.wait_ge(wvo_copied, 1)
                if b >= 1:
                    pe.wait_ge(z_copied, b)
                for i in range(2):
                    for k in range(DK):
                        o = b * SEQ + i * P
                        last = mm(pZ[:, i * D:(i + 1) * D], xT[:, k, o:o + P], wvo[:, k, :],
                                  start=k == 0, stop=k == DK - 1)
                last.then_inc(z_done, 1)
                pe.wait_ge(qk_copied, 2 * (b + 1))
                if b >= 2:
                    pe.wait_ge(exp_done, 2 * (b - 1))
                for i in range(2):
                    last = mm(pS[b % 2][:, i * SEQ:(i + 1) * SEQ], qk[:, b % 2, 0, i * P:(i + 1) * P],
                              qk[:, b % 2, 1, :], start=True, stop=True)
                last.then_inc(s_done, 1)

            def back(b):
                pe.wait_ge(exp_done, 2 * (b + 1))
                if b >= 1:
                    pe.wait_ge(aT_copied, b)
                for j in range(2):
                    for i in range(2):
                        last = tr(pT[:, j * SEQ + i * P:j * SEQ + (i + 1) * P],
                                  at[:, b % 2, i, j * P:(j + 1) * P], ident[:])
                last.then_inc(t_done, 1)
                pe.wait_ge(aT_copied, b + 1)
                pe.wait_ge(z_copied, b + 1)
                if b >= 1:
                    pe.wait_ge(o_read, 2 * b)
                for i in range(2):
                    for j in range(2):
                        last = mm(pO[:, i * D:(i + 1) * D], aT[:, b % 2, j, i * P:(i + 1) * P],
                                  zt[:, b % 2, j, :], start=j == 0, stop=j == 1)
                last.then_inc(o_done, 1)

            front(0)
            pe.wait_ge(d_xT, 16)
            for b in range(BATCH):
                if b + 1 < BATCH:
                    front(b + 1)
                back(b)

            def ctx_off(t):
                return pe.value_load(off1[0:1, t:t + 1], min_val=0, max_val=(E - 1) * DK * D)

            def tx(t):
                pe.wait_ge(d_rows[t], 16)
                if t >= 1:
                    pe.wait_ge(xlo_done, t)
                for k in range(DK):
                    last = tr(pX[:, k * P:(k + 1) * P], rows[:, t, k * P:(k + 1) * P], ident[:])
                last.then_inc(x_done, 1)

            def up(t):
                pe.wait_ge(xlo_done, t + 1)
                if t >= 1:
                    pe.wait_ge(h_done, t)
                off = ctx_off(t)
                for k in range(DK):
                    w = bass.ds(off + k * D, D)
                    last = split_mm(pG[:, 0:D], x1T(t, 0)[:, k * P:(k + 1) * P], x1T(t, 1)[:, k * P:(k + 1) * P],
                                    ctx_hi[:, w], ctx_lo[:, w], k == 0, k == DK - 1)
                last.then_inc(g_done, 1)

            def th(t):
                pe.wait_ge(h_done, t + 1)
                if t >= 1:
                    pe.wait_ge(hlo_done, t)
                for k in range(DK):
                    last = tr(pH[:, k * P:(k + 1) * P], hid[:, t % 2, k * P:(k + 1) * P], ident[:])
                last.then_inc(ht_done, 1)

            def down(t):
                pe.wait_ge(hlo_done, t + 1)
                if t >= 1:
                    pe.wait_ge(y_read, t)
                off = ctx_off(t)
                for k in range(DK):
                    w = bass.ds(off + k * D, D)
                    last = split_mm(pY[:, 0:D], hT[:, t % 2, 0, k * P:(k + 1) * P], hT[:, t % 2, 1, k * P:(k + 1) * P],
                                    ctx_hi[:, w], ctx_lo[:, w], k == 0, k == DK - 1)
                last.then_inc(y_done, 1)

            def tc(t):
                pe.wait_ge(x2_ready, t + 1)
                if t >= 1:
                    pe.wait_ge(c_copied, t)
                for k in range(DK):
                    last = tr(pC[:, k * P:(k + 1) * P], ring[:, (CHUNKS + t) % RING, k * P:(k + 1) * P], ident[:])
                last.then_inc(c_done, 1)

            def logits(t):
                pe.wait_ge(c_copied, t + 1)
                if t >= 1:
                    pe.wait_ge(mask_ready, t)
                for k in range(DK):
                    mm(pL[:, 0:E], x2T[:, k * P:(k + 1) * P], wr[:, k, :], start=k == 0, stop=False)
                mm(pL[:, 0:E], one_row[:], br[:], start=False, stop=True).then_inc(l_done, 1)

            def rank(t):
                pe.wait_ge(mask_ready, t + 1)
                if t >= 1:
                    pe.wait_ge(slot_ready, t)
                mm(pR[:, 0:E], below[:], m2[:, t, :], start=True, stop=False)
                mm(pR[:, 0:E], ones[:], m2cum[:, t, :], start=False, stop=True).then_inc(r_done, 1)

            pe.wait_ge(split_lo, CTX_PIECES)
            pe.wait_ge(tables, 1)
            pe.wait_ge(d_wr, 32)
            tx(0)
            for i in range(T + 4):
                for stage_of, t in ((tx, i + 1), (up, i), (down, i - 1), (logits, i - 3), (rank, i - 4),
                                    (tc, i - 2), (th, i)):
                    if 0 <= t < T and not (stage_of is tx and t == 0):
                        stage_of(t)
            pe.wait_ge(slot_ready, T)
            mm(pR[:, 0:E], ones[:], m2cum[:, T, :], start=True, stop=True).then_inc(n_done, 1)

            def ftx(t):
                pe.wait_ge(d_rows[t], 32)
                if t >= 2:
                    pe.wait_ge(xlo_done, T + t - 1)
                for k in range(DK):
                    last = tr(fX[t % 2][:, k * P:(k + 1) * P], rows[:, t, k * P:(k + 1) * P], ident[:])
                last.then_inc(x_done, 1)

            def w_off(t):
                return pe.value_load(off2[0:1, t:t + 1], min_val=0, max_val=(E - 1) * CHUNK)

            def fup(j):
                q, t = items[j]
                if t == 0:
                    pe.wait_ge(split_lo, CTX_PIECES + (q + 1) * Q_PIECES)
                if q == 0:
                    pe.wait_ge(xlo_done, T + t + 1)
                if j >= 2:
                    pe.wait_ge(h_done, T + j - 1)
                off = w_off(t)
                for k in range(DK):
                    w = bass.ds(off + ((q % 2) * E * CHUNK + k * 2 * FQ), 2 * FQ)
                    last = split_mm(fA[j % 2][:, :], x2s(t, 0)[:, k * P:(k + 1) * P], x2s(t, 1)[:, k * P:(k + 1) * P],
                                    w_hi[:, w], w_lo[:, w], k == 0, k == DK - 1)
                last.then_inc(g_done, 1)

            def fth(j):
                pe.wait_ge(h_done, T + j + 1)
                if j >= 2:
                    pe.wait_ge(hlo_done, T + j - 1)
                for k in range(FQ // P):
                    last = tr(fH[j % 2][:, k * P:(k + 1) * P], hid[:, (T + j) % 2, k * P:(k + 1) * P], ident[:])
                last.then_inc(ht_done, 1)

            def fdown(j):
                q, t = items[j]
                pe.wait_ge(hlo_done, T + j + 1)
                if j >= 2:
                    pe.wait_ge(y_read, T + j - 1)
                b = (T + j) % 2
                off = w_off(t)
                for k in range(FQ // P):
                    w = bass.ds(off + ((q % 2) * E * CHUNK + GU + k * D), D)
                    last = split_mm(fY[j % 2][:, 0:D], hT[:, b, 0, k * P:(k + 1) * P], hT[:, b, 1, k * P:(k + 1) * P],
                                    w_hi[:, w], w_lo[:, w], k == 0, k == FQ // P - 1)
                last.then_inc(y_done, 1)

            pe.wait_ge(tables, 2)
            ftx(0)
            ftx(1)
            for i in range(len(items) + 2):
                if i + 2 < T:
                    ftx(i + 2)
                if i < len(items):
                    fup(i)
                if 1 <= i <= len(items):
                    fth(i - 1)
                if i >= 2:
                    fdown(i - 2)

        @block.scalar
        def _(act):
            a = nc.scalar.activation
            act.dma_start(ids[:], ids_in).then_inc(d_ids, 16)

            def front(b):
                act.wait_ge(qk_done, b + 1)
                if b >= 2:
                    act.wait_ge(s_done, b - 1)
                for w in range(2):
                    a(qk[:, b % 2, w, :], pQK[w * RANK:(w + 1) * RANK, 0:SEQ], ACT.Copy).then_inc(qk_copied, 1)
                act.wait_ge(z_done, b + 1)
                if b >= 2:
                    act.wait_ge(o_done, b - 1)
                a(zt[:, b % 2, :, :].rearrange("p c d -> p (c d)"), pZ[:, :], ACT.Copy).then_inc(z_copied, 1)

            def exps(b):
                act.wait_ge(negmax_ready, b + 1)
                if b >= 2:
                    act.wait_ge(t_done, b - 1)
                for i in range(2):
                    a(at[:, b % 2, i, :], pS[b % 2][:, i * SEQ:(i + 1) * SEQ], ACT.Exp, bias=negmax[:, b % 2, i:i + 1],
                      accum_out=esum[:, b % 2, i:i + 1]).then_inc(exp_done, 1)

            def split(k):
                n, _, src, hi, _ = all_pieces[k]
                act.wait_ge(d_chunk[n % SLOTS], 16 * (n // SLOTS + 1))
                if n >= chunk_of(2, 0):
                    act.wait_ge(y_done, T + ((n - N_CTX) // E - 1) * T)
                a(hi, src, ACT.Copy).then_inc(split_hi, 1)

            front(0)
            exps(0)
            done = 0
            for b in range(BATCH):
                if b + 1 < BATCH:
                    front(b + 1)
                    exps(b + 1)
                act.wait_ge(t_done, b + 1)
                if b >= 2:
                    act.wait_ge(o_done, b - 1)
                a(aT[:, b % 2, :, :].rearrange("p j i -> p (j i)"), pT[:, :], ACT.Copy).then_inc(aT_copied, 1)
                split(done)
                done += 1

            def xhi(t):
                act.wait_ge(x_done, t + 1)
                if t >= 2:
                    act.wait_ge(g_done, t - 1)
                a(x1T(t, 0), pX[:, 0:D], ACT.Copy).then_inc(xhi_done, 1)

            def silu(t):
                act.wait_ge(g_done, t + 1)
                if t >= 2:
                    act.wait_ge(h_done, t - 1)
                a(gate[:, t % 2, :], pG[:, 0:D], ACT.Silu).then_inc(silu_done, 1)

            def evac(t):
                act.wait_ge(c_done, t + 1)
                if t >= 1:
                    act.wait_ge(l_done, t)
                a(x2T[:], pC[:, 0:D], ACT.Copy).then_inc(c_copied, 1)

            def hhi(t):
                act.wait_ge(ht_done, t + 1)
                if t >= 2:
                    act.wait_ge(y_done, t - 1)
                a(hT[:, t % 2, 0, :], pH[:, 0:D], ACT.Copy).then_inc(hhi_done, 1)

            xhi(0)
            for i in range(T + 2):
                for stage_of, t in ((xhi, i + 1), (silu, i), (evac, i - 2), (hhi, i)):
                    if 0 <= t < T and not (stage_of is xhi and t == 0):
                        stage_of(t)
                if done < CTX_PIECES + Q_PIECES:
                    split(done)
                    done += 1

            def fxhi(t):
                act.wait_ge(x_done, T + t + 1)
                if t == 0:
                    act.wait_ge(y_done, T)
                a(x2s(t, 0), fX[t % 2][:, 0:D], ACT.Copy).then_inc(xhi_done, 1)

            def fsilu(j):
                act.wait_ge(g_done, T + j + 1)
                act.wait_ge(h_done, T + j - 1)
                a(gate[:, (T + j) % 2, :], fA[j % 2][:, 0:FQ], ACT.Silu).then_inc(silu_done, 1)

            def fhhi(j):
                act.wait_ge(ht_done, T + j + 1)
                act.wait_ge(y_done, T + j - 1)
                a(hT[:, (T + j) % 2, 0, :], fH[j % 2][:, 0:FQ], ACT.Copy).then_inc(hhi_done, 1)

            fxhi(0)
            fxhi(1)
            for i in range(len(items) + 1):
                if i + 2 < T:
                    fxhi(i + 2)
                if i < len(items):
                    fsilu(i)
                if i >= 1:
                    fhhi(i - 1)
                if i < len(items):
                    q, t = items[i]
                    if q + 1 < NQ:
                        for k in quarter_pieces(q + 1, t):
                            split(k)
                if i == 3 * T:
                    a(lexp[:], rows[:, :, LOG:LOG + E], ACT.Exp).then_inc(lexp_done, 1)

        @block.vector
        def _(dve):
            v = nc.vector
            steps = [0]

            def step(ins):
                steps[0] += 1
                ins.then_inc(dve_step, 1)
                dve.wait_ge(dve_step, steps[0])

            def tile_tables(count_bank, col):
                step(v.tensor_tensor(out=gt[:], in0=count_bank[:, col:col + E].unsqueeze(2).broadcast_to([P, E, CHUNKS]),
                                     in1=fill[:], op=ALU.is_gt))
                step(v.tensor_reduce(out=ntile[:], in_=gt[:], axis=AX.X, op=ALU.add))
                for e in range(1, E):
                    step(v.tensor_tensor(out=first[:, e:e + 1], in0=first[:, e - 1:e], in1=ntile[:, e - 1:e], op=ALU.add))
                step(v.tensor_tensor(out=past[:], in0=tile_no[:].unsqueeze(2).broadcast_to([P, T, E]),
                                     in1=first[:].unsqueeze(1).broadcast_to([P, T, E]), op=ALU.is_ge))
                step(v.tensor_reduce(out=expert[:], in_=past[:, :, 1:E], axis=AX.X, op=ALU.add))

            step(v.memset(first[:], 0.0))
            step(v.memset(m1cum[:], 0.0))
            step(v.memset(m2cum[:], 0.0))
            step(v.memset(ge1[:], 0.0))
            step(v.memset(ge1[:, 0, :], 1.0))
            dve.wait_ge(d_ids, 16)
            step(v.tensor_copy(idf[:], ids[:]))
            for e in range(1, E):
                step(v.tensor_scalar(out=ge1[:, e, :], in0=idf[:], scalar1=float(e * PER_EXPERT), scalar2=None,
                                     op0=ALU.is_ge))
            step(v.tensor_tensor(out=m1[:].rearrange("p c e -> p e c"), in0=ge1[:, 0:E, :], in1=ge1[:, 1:E + 1, :],
                                 op=ALU.subtract))
            for c in range(CHUNKS):
                v.tensor_tensor(out=m1cum[:, c + 1, :], in0=m1cum[:, c, :], in1=m1[:, c, :],
                                op=ALU.add).then_inc(m1_ready, 1)
                dve.wait_ge(m1_ready, c + 1)
            dve.wait_ge(wvo_done, 1)
            v.tensor_copy(wvo.rearrange("p k n -> p (k n)"), pW[:, :]).then_inc(wvo_copied, 1)
            dve.wait_ge(consts, 13)
            dve.wait_ge(r1_done, 1)
            tile_tables(pR1, 64)
            v.tensor_scalar(out=off1[:], in0=expert[:], scalar1=float(DK * D), scalar2=None,
                            op0=ALU.mult).then_inc(tables, 1)
            step(v.tensor_scalar(out=first128[:], in0=first[:], scalar1=float(P), scalar2=None, op0=ALU.mult))
            step(v.tensor_tensor(out=pos1[:], in0=pR1[:, 0:CHUNKS * E].rearrange("p (c e) -> p c e", e=E),
                                 in1=first128[:].unsqueeze(1).broadcast_to([P, CHUNKS, E]), op=ALU.add))
            step(v.tensor_tensor(out=pos1[:], in0=pos1[:], in1=m1[:], op=ALU.mult))
            step(v.tensor_reduce(out=slot1f[:], in_=pos1[:], axis=AX.X, op=ALU.add))
            v.tensor_copy(slot1[:], slot1f[:]).then_inc(route1, 1)

            def maxes(b):
                dve.wait_ge(s_done, b + 1)
                step(v.reduce_max(negmax[:, b % 2, :], pS[b % 2][:, :].rearrange("p (i j) -> p i j", i=2), AX.X))
                v.tensor_scalar(out=negmax[:, b % 2, :], in0=negmax[:, b % 2, :], scalar1=-1.0, scalar2=None,
                                op0=ALU.mult).then_inc(negmax_ready, 1)

            def norm(n, buf, i, row, done):
                dve.wait_ge(rstd_ready, n + 1)
                v.tensor_scalar(out=row, in0=row, scalar1=mv[:, buf, i, 0:1], scalar2=rstd[:, buf, i:i + 1],
                                op0=ALU.subtract, op1=ALU.mult).then_inc(done, 1)

            def moments(buf, width, rowsof):
                for i in range(width):
                    step(v.bn_stats(stats[:, i, :], rowsof[i]))
                for i in range(width):
                    step(v.bn_aggr(mv[:, buf, i, :], stats[:, i, :]))
                v.tensor_scalar(out=mv[:, buf, 0:width, 1], in0=mv[:, buf, 0:width, 1], scalar1=EPS, scalar2=None,
                                op0=ALU.add).then_inc(var_ready, 1)

            maxes(0)
            dve.wait_ge(d_x, 16)
            for b in range(BATCH):
                if b + 1 < BATCH:
                    maxes(b + 1)
                dve.wait_ge(o_done, b + 1)
                step(v.reciprocal(rinv[:, b % 2, :], esum[:, b % 2, :]))
                for i in range(2):
                    c = 2 * b + i
                    if c >= RING:
                        dve.wait_ge(*scat(c - RING))
                    v.tensor_copy(ring[:, c % RING, TOK:TOK + 1], tok[:, c:c + 1])
                    v.memset(ring[:, c % RING, LOG:ROW], 0.0)
                    v.scalar_tensor_tensor(out=ring[:, c % RING, 0:D], in0=pO[:, i * D:(i + 1) * D],
                                           scalar=rinv[:, b % 2, i:i + 1], in1=xn[:, c, :],
                                           op0=ALU.mult, op1=ALU.add).then_inc(o_read, 1)
                dve.wait_ge(o_read, 2 * (b + 1))
                moments(b % 2, 2, [ring[:, (2 * b + i) % RING, 0:D] for i in range(2)])
                for i in range(2):
                    norm(LN1 + b, b % 2, i, ring[:, (2 * b + i) % RING, 0:D], row_ready)

            def ring_of(t):
                return (CHUNKS + t) % RING

            def xlo(t):
                dve.wait_ge(xhi_done, t + 1)
                if t >= 2:
                    dve.wait_ge(g_done, t - 1)
                v.tensor_tensor(out=x1T(t, 1), in0=pX[:, 0:D], in1=x1T(t, 0).bitcast(F32),
                                op=ALU.subtract).then_inc(xlo_done, 1)

            def hidden(t):
                dve.wait_ge(silu_done, t + 1)
                if t >= 2:
                    dve.wait_ge(ht_done, t - 1)
                v.tensor_tensor(out=hid[:, t % 2, :], in0=pG[:, 0:D], in1=gate[:, t % 2, :],
                                op=ALU.mult).then_inc(h_done, 1)

            def hlo(t):
                dve.wait_ge(hhi_done, t + 1)
                v.tensor_tensor(out=hT[:, t % 2, 1, :], in0=pH[:, 0:D], in1=hT[:, t % 2, 0, :].bitcast(F32),
                                op=ALU.subtract).then_inc(hlo_done, 1)

            def resid(t):
                dve.wait_ge(y_done, t + 1)
                dve.wait_ge(*scat(CHUNKS + t - RING))
                r = ring[:, ring_of(t), 0:D]
                ins = v.tensor_tensor(out=r, in0=pY[:, 0:D], in1=rows[:, t, 0:D], op=ALU.add)
                ins.then_inc(y_read, 1)
                dve.wait_ge(y_read, t + 1)
                v.tensor_copy(ring[:, ring_of(t), TOK:TOK + 1], rows[:, t, TOK:TOK + 1])
                moments(t % 2, 1, [r])

            def norm2(t):
                norm(LN2 + t, t % 2, 0, ring[:, ring_of(t), 0:D], x2_ready)

            def validity():
                for t in range(T):
                    dve.wait_ge(d_rows[t], 16)
                step(v.tensor_scalar(out=valid[:], in0=rows[:, :, TOK], scalar1=float(TOKENS), scalar2=None,
                                     op0=ALU.is_lt))
                step(v.tensor_scalar(out=far[:], in0=valid[:], scalar1=-FAR, scalar2=FAR, op0=ALU.mult, op1=ALU.add))

            def mask(t):
                dve.wait_ge(l_done, t + 1)
                step(v.reduce_max(lmax[:], pL[:, 0:E], AX.X))
                lm = ring[:, ring_of(t), LOG:LOG + E]
                step(v.tensor_scalar(out=lm, in0=pL[:, 0:E], scalar1=lmax[:], scalar2=None, op0=ALU.subtract))
                step(v.scalar_tensor_tensor(out=lw[:], in0=lm, scalar=0.0, in1=prio[:], op0=ALU.is_ge, op1=ALU.mult))
                step(v.reduce_max(lwmax[:], lw[:], AX.X))
                step(v.tensor_scalar(out=m2[:, t, :], in0=lw[:], scalar1=lwmax[:], scalar2=valid[:, t:t + 1],
                                     op0=ALU.is_equal, op1=ALU.mult))
                v.tensor_tensor(out=m2cum[:, t + 1, :], in0=m2cum[:, t, :], in1=m2[:, t, :],
                                op=ALU.add).then_inc(mask_ready, 1)

            def slot(t):
                dve.wait_ge(r_done, t + 1)
                step(v.tensor_tensor(out=pos2[:, 0, :], in0=pR[:, 0:E], in1=base2[:], op=ALU.add))
                step(v.tensor_tensor(out=pos2[:, 1, :], in0=pos2[:, 0, :], in1=m2[:, t, :], op=ALU.mult))
                step(v.reduce_sum(slot2f[:, t:t + 1], pos2[:, 1, :], AX.X))
                v.tensor_scalar(out=slot2[:, t:t + 1], in0=slot2f[:, t:t + 1], scalar1=far[:, t:t + 1], scalar2=None,
                                op0=ALU.add).then_inc(slot_ready, 1)

            xlo(0)
            for i in range(T + 4):
                if i == 3:
                    validity()
                for stage_of, t in ((xlo, i + 1), (hidden, i), (resid, i - 1), (hlo, i), (norm2, i - 1),
                                    (mask, i - 3), (slot, i - 4)):
                    if 0 <= t < T and not (stage_of is xlo and t == 0):
                        stage_of(t)

            dve.wait_ge(n_done, 1)
            tile_tables(pR, 0)
            step(v.tensor_scalar(out=off2[:], in0=expert[:], scalar1=float(CHUNK), scalar2=None, op0=ALU.mult))
            step(v.tensor_tensor(out=pastf[:], in0=past[:], in1=first[:].unsqueeze(1).broadcast_to([P, T, E]), op=ALU.mult))
            step(v.reduce_max(begun[:], pastf[:], AX.X))
            step(v.tensor_tensor(out=begun[:], in0=tile_no[:], in1=begun[:], op=ALU.subtract))
            step(v.scalar_tensor_tensor(out=blk[:], in0=expert[:], scalar=float(REGION // P), in1=begun[:],
                                        op0=ALU.mult, op1=ALU.add))
            v.tensor_scalar(out=row2[:], in0=blk[:], scalar1=float(P), scalar2=None, op0=ALU.mult).then_inc(tables, 1)

            def fxlo(t):
                dve.wait_ge(xhi_done, T + t + 1)
                v.tensor_tensor(out=x2s(t, 1), in0=fX[t % 2][:, 0:D], in1=x2s(t, 0).bitcast(F32),
                                op=ALU.subtract).then_inc(xlo_done, 1)

            def fhidden(j):
                dve.wait_ge(silu_done, T + j + 1)
                dve.wait_ge(ht_done, T + j - 1)
                v.tensor_tensor(out=hid[:, (T + j) % 2, :], in0=fA[j % 2][:, FQ:2 * FQ], in1=gate[:, (T + j) % 2, :],
                                op=ALU.mult).then_inc(h_done, 1)

            def fhlo(j):
                dve.wait_ge(hhi_done, T + j + 1)
                v.tensor_tensor(out=hT[:, (T + j) % 2, 1, :], in0=fH[j % 2][:, 0:FQ],
                                in1=hT[:, (T + j) % 2, 0, :].bitcast(F32), op=ALU.subtract).then_inc(hlo_done, 1)

            def fsum(j):
                q, t = items[j]
                dve.wait_ge(y_done, T + j + 1)
                if q == 0:
                    v.tensor_copy(acc[:, t, :], fY[j % 2][:, 0:D]).then_inc(y_read, 1)
                else:
                    v.tensor_tensor(out=acc[:, t, :], in0=fY[j % 2][:, 0:D], in1=acc[:, t, :],
                                    op=ALU.add).then_inc(y_read, 1)

            def gates():
                dve.wait_ge(lexp_done, 1)
                step(v.reduce_sum(lsum[:], lexp[:], AX.X))
                step(v.reciprocal(topw[:], lsum[:]))
                step(v.tensor_copy(outidx[:], rows[:, :, TOK]))

            def finish(t):
                n = CHUNKS + T + t
                dve.wait_ge(*scat(n - RING))
                dve.wait_ge(y_read, T + 3 * T + t + 1)
                r = ring[:, n % RING, 0:D]
                step(v.scalar_tensor_tensor(out=r, in0=acc[:, t, :], scalar=topw[:, t:t + 1], in1=rows[:, t, 0:D],
                                            op0=ALU.mult, op1=ALU.add))
                moments(t % 2, 1, [r])

            def finish_norm(t):
                norm(LN3 + t, t % 2, 0, ring[:, (CHUNKS + T + t) % RING, 0:D], out_ready)

            fxlo(0)
            fxlo(1)
            for i in range(len(items) + 3):
                if i + 2 < T:
                    fxlo(i + 2)
                if i < len(items):
                    fhidden(i)
                if 1 <= i <= len(items):
                    fhlo(i - 1)
                if 2 <= i <= len(items) + 1:
                    fsum(i - 2)
                if i == 3 * T + 1:
                    gates()
                if i - 2 >= 3 * T and i - 2 < len(items):
                    finish(i - 2 - 3 * T)
                if i - 3 >= 3 * T:
                    finish_norm(i - 3 - 3 * T)


def kernel(**inputs):
    import concourse.bacc as bacc
    from concourse.bass_utils import run_bass_kernel_spmd

    def rows_first(a, k):
        n = a.shape[-1]
        return np.ascontiguousarray(a.reshape(k, P, n).transpose(1, 0, 2).reshape(P, k * n))

    x = np.asarray(inputs["x"]).reshape(TOKENS, D)
    wq, wk = np.asarray(inputs["L0_attn_Wq"]), np.asarray(inputs["L0_attn_Wk"])
    wv, wo = np.asarray(inputs["L0_attn_Wv"]), np.asarray(inputs["L0_attn_Wo"])
    ctx = np.asarray(inputs["ctx_2048"])
    wg, wu, wd = (np.asarray(inputs[f"L0_ffn_W{c}"]) for c in "gud")
    aw = np.concatenate([rows_first(np.concatenate([wq, wk], 0).T, DK), rows_first(wv, DK), rows_first(wo.T, DK)], 1)
    ctxT = np.concatenate([rows_first(ctx[e].T, DK) for e in range(E)], 1)
    chunks = []
    for q in range(NQ):
        f = slice(q * FQ, (q + 1) * FQ)
        for e in range(E):
            gu = rows_first(np.concatenate([wg[e][:, f], wu[e][:, f]], 1), DK)
            chunks.append(np.concatenate([gu, rows_first(wd[e][f, :], FQ // P)], 1))
    arrays = {
        "in_attn_w": np.ascontiguousarray(aw),
        "in_xT": rows_first(x.T, DK),
        "in_x_tok": rows_first(x, CHUNKS),
        "in_ids": np.ascontiguousarray(np.asarray(inputs["itok_BxS_13_99985"]).reshape(CHUNKS, P).T),
        "in_wr": rows_first(np.asarray(inputs["L0_ffn_Wr"]), DK),
        "in_br": np.ascontiguousarray(np.asarray(inputs["L0_ffn_br"]).reshape(1, E)),
        "in_ctxT": np.ascontiguousarray(ctxT),
        "in_w_ffn": np.ascontiguousarray(np.stack(chunks)),
    }
    nc = bacc.Bacc("TRN2", target_bir_lowering=False, num_devices=1)
    args = [nc.dram_tensor(n, a.shape, mybir.dt.from_np(a.dtype), kind="ExternalInput").ap() for n, a in arrays.items()]
    out = nc.dram_tensor("out_tokens", (TOKENS, D), F32, kind="ExternalOutput").ap()
    route_kernel(nc, *args, out)
    got = run_bass_kernel_spmd(nc, [arrays], core_ids=[0]).results[0]["out_tokens"]
    return got.reshape(BATCH, SEQ, D)
```

```python
from contextlib import ExitStack

import numpy as np
import concourse.bass as bass
from concourse import mybir

ALU = mybir.AluOpType
ACT = mybir.ActivationFunctionType
AX = mybir.AxisListType
F32 = mybir.dt.float32
F32R = mybir.dt.float32r
BF16 = mybir.dt.bfloat16
I32 = mybir.dt.int32

P = 128
D = 256
DK = D // P
BATCH, SEQ = 4, 256
TOKENS = BATCH * SEQ
CHUNKS = TOKENS // P
RANK = 64
E = 4
VOCAB = 12500
PER_EXPERT = VOCAB // E
F = 1024
NQ = 4
FQ = F // NQ
T = (TOKENS + E * (P - 1)) // P
EPS = 1e-5
FAR = float(1 << 20)

TOK, LOG, ROW = D, D + 1, 264
QKW = DK * 2 * RANK
REGION = TOKENS
BLOCKS2 = (E - 1) * (REGION // P) + T
RING = 6
PIECE = 512
GU = DK * 2 * FQ
CHUNK = GU + (FQ // P) * D
SLOTS = 3
CTX_CHUNK = (E // 2) * DK * D
CW = E + D + E
N_CTX = 2


def route_kernel(nc, aw, xT_in, x_in, ids_in, wr_in, br_in, ctx_in, ctxn_in, wffn_in, out):
    scr1 = nc.dram_tensor("x1_sorted", (T * P, ROW), F32).ap()
    scr2 = nc.dram_tensor("x2_sorted", (BLOCKS2 * P, ROW), F32).ap()

    with ExitStack() as ctx:
        def sb(name, shape, dt=F32):
            return ctx.enter_context(nc.sbuf_tensor(name, shape, dt))

        def sem(name):
            return ctx.enter_context(nc.semaphore(name))

        w_hi = sb("w_hi", [P, 2 * E * CHUNK], F32R)
        w_lo = sb("w_lo", [P, 2 * E * CHUNK], F32R)
        xr = sb("xr", [P, T * 2 * D], F32R)
        hT = sb("hT", [P, 2, 2, FQ], F32R)
        stage = sb("stage", [P, SLOTS, CHUNK])
        arena = sb("arena", [P, 9984])
        rows = sb("rows", [P, T, ROW])
        ring = sb("ring", [P, RING, ROW])
        gate = sb("gate", [P, 2, FQ])
        hid = sb("hid", [P, 2, FQ])
        ones_f = sb("ones_f", [P, P])
        wrc = sb("wrc", [P, DK, E])
        br_all = sb("br_all", [P, E])
        x1logit = sb("x1logit", [P, 2, E])
        rawlogit = sb("rawlogit", [P, 2, E])
        logit = sb("logit", [P, E])
        nmr = sb("nmr", [P, 2])
        fill2 = sb("fill2", [P, E, CHUNKS])
        padrow = sb("padrow", [P, ROW])
        ident = sb("ident", [P, P])
        below = sb("below", [P, P], BF16)
        ones = sb("ones", [P, P], BF16)
        ids = sb("ids", [P, CHUNKS], I32)
        wr = sb("wr", [P, DK, E])
        br = sb("br", [1, E])
        one_row = sb("one_row", [1, P])
        tok = sb("tok", [P, CHUNKS])
        tile_no = sb("tile_no", [P, T])
        fill = sb("fill", [P, E, CHUNKS])
        prio = sb("prio", [P, E])
        base2 = sb("base2", [P, E])
        mhalf = sb("mhalf", [P, 2])
        idf = sb("idf", [P, CHUNKS])
        ge1 = sb("ge1", [P, E + 1, CHUNKS])
        m1 = sb("m1", [P, CHUNKS, E], BF16)
        m1cum = sb("m1cum", [P, CHUNKS + 1, E], BF16)
        pos1 = sb("pos1", [P, CHUNKS, E])
        slot1f = sb("slot1f", [P, CHUNKS])
        slot1 = sb("slot1", [P, CHUNKS], I32)
        m2 = sb("m2", [P, T, E], BF16)
        m2cum = sb("m2cum", [P, T + 1, E], BF16)
        pos2 = sb("pos2", [P, E])
        slot2f = sb("slot2f", [P, T])
        slot2 = sb("slot2", [P, T], I32)
        valid = sb("valid", [P, T])
        far = sb("far", [P, T])
        gt = sb("gt", [P, E, CHUNKS])
        ntile = sb("ntile", [P, E])
        first = sb("first", [P, E])
        first128 = sb("first128", [P, E])
        past = sb("past", [P, T, E])
        pastf = sb("pastf", [P, T, E])
        expert = sb("expert", [P, T])
        begun = sb("begun", [P, T])
        blk = sb("blk", [P, T])
        off1 = sb("off1", [P, T], I32)
        off2 = sb("off2", [P, T], I32)
        row2 = sb("row2", [P, T], I32)
        outidx = sb("outidx", [P, T], I32)
        negmax = sb("negmax", [P, 2, 2])
        esum = sb("esum", [P, 2, 2])
        rinv = sb("rinv", [P, 2, 2])
        stats = sb("stats", [P, 2, 6])
        mv = sb("mv", [P, 2, 2, 2])
        rstd = sb("rstd", [P, 2, 2])
        lmax = sb("lmax", [P, 1])
        lw = sb("lw", [P, E])
        lwmax = sb("lwmax", [P, 1])
        lexp = sb("lexp", [P, T, E])
        lsum = sb("lsum", [P, T])
        topw = sb("topw", [P, T])

        cut = [0]

        def carve(n):
            cut[0] += n
            return arena[:, cut[0] - n:cut[0]]

        xT = carve(DK * TOKENS).rearrange("p (k n) -> p k n", k=DK)
        xn = carve(CHUNKS * D).rearrange("p (c d) -> p c d", c=CHUNKS)
        awt = carve(DK * (2 * RANK + 2 * D))
        wqk = awt[:, 0:DK * 2 * RANK].rearrange("p (k n) -> p k n", k=DK)
        wv = awt[:, 256:256 + DK * D].rearrange("p (k n) -> p k n", k=DK)
        woT = awt[:, 768:768 + DK * D].rearrange("p (k n) -> p k n", k=DK)
        wvo = carve(DK * D).rearrange("p (k n) -> p k n", k=DK)
        zt = carve(2 * 2 * D).rearrange("p (b c d) -> p b c d", b=2, c=2)
        at = carve(2 * 2 * SEQ).rearrange("p (b i j) -> p b i j", b=2, i=2)
        aT = carve(2 * 2 * SEQ).rearrange("p (b j i) -> p b j i", b=2, j=2)
        qk = carve(2 * 2 * SEQ).rearrange("p (b w i) -> p b w i", b=2, w=2)[0:RANK]
        acc = arena[:, 0:T * D].rearrange("p (t d) -> p t d", t=T)

        X1T = 2 * E * DK * CW
        ctx_hi, ctx_lo = xr[:, 0:X1T // 2], xr[:, X1T // 2:X1T]
        ctx_hi4, ctx_lo4 = (c.rearrange("p (e k n) -> p e k n", e=E, k=DK) for c in (ctx_hi, ctx_lo))
        ctxn = w_hi[:, E * CHUNK:E * CHUNK + E * DK * D].bitcast(F32).rearrange("p (e k f) -> p e k f", e=E, k=DK)

        def x1T(t, part):
            o = X1T + (t % 2) * 2 * D + part * D
            return xr[:, o:o + D]

        def x2s(t, part):
            o = t * 2 * D + part * D
            return xr[:, o:o + D]

        bank = [ctx.enter_context(nc.psum_tensor(f"bank{i}", [P, 512], F32)) for i in range(8)]
        pQK, pZ, pS, pT, pO, pR1, pW = bank[0], bank[1], bank[2:4], bank[4], bank[5], bank[6], bank[7]
        pX, pG, pH, pY, pL, pR = bank[0], bank[1], bank[2], bank[3], bank[5], bank[6]
        pWrSum, pBr, pM = pO[:, 0:E], pO[:, 8:8 + E], pR1[:, 160:160 + E * DK * E]
        fX = [bank[0], bank[7]]
        fA, fH, fY = [bank[1], bank[5]], [bank[2], bank[6]], [bank[3], bank[4]]

        d_aqk, d_avo, d_xT0, d_xT, d_x, d_ids, d_wr = (
            sem(n) for n in ("d_aqk", "d_avo", "d_xT0", "d_xT", "d_x", "d_ids", "d_wr"))
        d_init1, d_init2 = sem("d_init1"), sem("d_init2")
        d_chunk = [sem(f"d_chunk{i}") for i in range(SLOTS)]
        d_rows = [sem(f"d_rows{t}") for t in range(T)]
        d_scat = [sem(f"d_scat{i}") for i in range(RING)]
        consts = sem("consts")
        pad_ready = sem("pad_ready")
        wvo_done, wvo_copied = sem("wvo_done"), sem("wvo_copied")
        m1_ready, r1_done, route1 = sem("m1_ready"), sem("r1_done"), sem("route1")
        qk_done, z_done, s_done, t_done, o_done = (sem(n) for n in ("qk_done", "z_done", "s_done", "t_done", "o_done"))
        qk_copied, z_copied, exp_done, aT_copied = (sem(n) for n in ("qk_copied", "z_copied", "exp_done", "aT_copied"))
        negmax_ready, o_read = sem("negmax_ready"), sem("o_read")
        var_ready, rstd_ready, row_ready = sem("var_ready"), sem("rstd_ready"), sem("row_ready")
        split_hi, split_lo = sem("split_hi"), sem("split_lo")
        dve_step = sem("dve_step")
        x_done, xhi_done, xlo_done, g_done = (sem(n) for n in ("x_done", "xhi_done", "xlo_done", "g_done"))
        silu_done, h_done, ht_done, hhi_done, hlo_done = (
            sem(n) for n in ("silu_done", "h_done", "ht_done", "hhi_done", "hlo_done"))
        y_done, y_read = sem("y_done"), sem("y_read")
        d_ctxn = sem("d_ctxn")
        br_done, wrc_ready, m_done, router_hi, router_lo = (
            sem(n) for n in ("br_done", "wrc_ready", "m_done", "router_hi", "router_lo"))
        x2_ready, nmr_ready = sem("x2_ready"), sem("nmr_ready")
        mask_ready, r_done, slot_ready = (sem(n) for n in ("mask_ready", "r_done", "slot_ready"))
        n_done, tables = sem("n_done"), sem("tables")
        lexp_done = sem("lexp_done")
        out_ready = sem("out_ready")

        LN1, LN2, LN3 = 0, BATCH, BATCH + T

        def scat(n):
            return d_scat[n % RING], 16 * (n // RING + 1)

        def pieces(n):
            return CTX_CHUNK // PIECE if n < N_CTX else CHUNK // PIECE

        def pieces_to(n):
            return sum(pieces(i) for i in range(n))

        def chunk_of(q, e):
            return N_CTX + q * E + e

        def piece_list(n):
            got = []
            for i in range(pieces(n)):
                src = stage[:, n % SLOTS, i * PIECE:(i + 1) * PIECE]
                if n < N_CTX:
                    e = n * (E // 2) + i
                    got.append((src.rearrange("p (k d) -> p k d", k=DK), ctx_hi4[:, e, :, E:E + D],
                                ctx_lo4[:, e, :, E:E + D]))
                else:
                    q, e = divmod(n - N_CTX, E)
                    o = ((q % 2) * E + e) * CHUNK + i * PIECE
                    got.append((src, w_hi[:, o:o + PIECE], w_lo[:, o:o + PIECE]))
            return got

        all_pieces = [(n, i) + p for n in range(N_CTX + NQ * E) for i, p in enumerate(piece_list(n))]
        CTX_PIECES = pieces_to(N_CTX)
        Q_PIECES = E * pieces(N_CTX)
        GAP_PIECES = 4
        share = [0, 1, 1, 2, 1, 2, 1, 2, 1, 1, 0]
        assert sum(share) == Q_PIECES and len(share) == T

        def quarter_pieces(q, t):
            a = CTX_PIECES + q * Q_PIECES + sum(share[:t])
            return range(a, a + share[t])

        items = [(q, t) for q in range(NQ) for t in range(T)]
        block = ctx.enter_context(nc.Block())

        @block.sync
        def _(sp):
            xT_rows = xT_in.rearrange("p (k n) -> p k n", k=DK)
            sp.dma_start(awt[:, 0:QKW], aw[:, 0:QKW]).then_inc(d_aqk, 16)
            sp.dma_start(xT[:, :, 0:SEQ], xT_rows[:, :, 0:SEQ]).then_inc(d_xT0, 16)
            sp.dma_start(awt[:, QKW:], aw[:, QKW:]).then_inc(d_avo, 16)
            sp.dma_start(xT[:, :, SEQ:], xT_rows[:, :, SEQ:]).then_inc(d_xT, 16)
            sp.wait_ge(pad_ready, 1)
            sp.dma_start(scr1.rearrange("(p r) c -> p r c", p=P),
                         padrow[:].unsqueeze(1).broadcast_to([P, T, ROW])).then_inc(d_init1, 16)
            sp.dma_start(xn, x_in.rearrange("p (c d) -> p c d", c=CHUNKS)).then_inc(d_x, 16)

            def load_chunk(n):
                if n >= SLOTS:
                    sp.wait_ge(split_lo, pieces_to(n - SLOTS + 1))
                src = ctx_in[:, n * CTX_CHUNK:(n + 1) * CTX_CHUNK] if n < N_CTX else wffn_in[n - N_CTX]
                sp.dma_start(stage[:, n % SLOTS, 0:pieces(n) * PIECE], src).then_inc(d_chunk[n % SLOTS], 16)

            for n in range(SLOTS):
                load_chunk(n)
            sp.dma_start(ctxn, ctxn_in.rearrange("p (e k f) -> p e k f", e=E, k=DK)).then_inc(d_ctxn, 16)
            sp.dma_start(scr2.rearrange("(p r) c -> p r c", p=P),
                         padrow[:].unsqueeze(1).broadcast_to([P, BLOCKS2, ROW])).then_inc(d_init2, 16)
            load_chunk(SLOTS)
            for n in range(CHUNKS):
                sp.wait_ge(*scat(n))
            for t in range(T):
                sp.dma_start(rows[:, t, :], scr1[t * P:(t + 1) * P, :]).then_inc(d_rows[t], 16)
            for n in range(SLOTS + 1, N_CTX + E + 1):
                load_chunk(n)
            def first_row(t):
                return sp.value_load(row2[0:1, t:t + 1], min_val=0, max_val=(BLOCKS2 - 1) * P)

            sp.wait_ge(tables, 2)
            r = first_row(0)
            for n in range(CHUNKS, CHUNKS + T):
                sp.wait_ge(*scat(n))
            for t in range(T):
                if t >= 1:
                    r = first_row(t)
                sp.dma_start(rows[:, t, :], scr2[bass.ds(r, P), :]).then_inc(d_rows[t], 16)
            for n in range(N_CTX + E + 1, N_CTX + NQ * E):
                load_chunk(n)
            for n in range(CHUNKS + T, CHUNKS + 2 * T):
                sp.wait_ge(*scat(n))

        @block.gpsimd
        def _(pool):
            def const(ins):
                ins.then_inc(consts, 1)
                const.n += 1
            const.n = 0
            g = nc.gpsimd
            const(g.memset(padrow[:], 0.0))
            const(g.memset(ident[:], 1.0))
            const(g.memset(below[:], 1.0))
            const(g.memset(ones[:], 1.0))
            const(g.memset(one_row[:], 1.0))
            const(g.memset(ones_f[:], 1.0))
            const(g.memset(mhalf[:], -0.5))
            const(g.iota(tok[:], pattern=[[P, CHUNKS]], base=0, channel_multiplier=1,
                         allow_small_or_imprecise_dtypes=True))
            const(g.iota(tile_no[:], pattern=[[1, T]], base=0, channel_multiplier=0,
                         allow_small_or_imprecise_dtypes=True))
            const(g.iota(fill[:], pattern=[[0, E], [P, CHUNKS]], base=0, channel_multiplier=0,
                         allow_small_or_imprecise_dtypes=True))
            const(g.iota(prio[:], pattern=[[-1, E]], base=E, channel_multiplier=0,
                         allow_small_or_imprecise_dtypes=True))
            const(g.iota(base2[:], pattern=[[REGION, E]], base=0, channel_multiplier=0,
                         allow_small_or_imprecise_dtypes=True))
            pool.wait_ge(consts, const.n)
            g.memset(padrow[:, TOK:TOK + 1], FAR).then_inc(pad_ready, 1)
            const(g.affine_select(out=ident[:], in_=ident[:], compare_op=ALU.is_equal, fill=0.0, base=0,
                                  pattern=[[-1, P]], channel_multiplier=1))
            const(g.affine_select(out=below[:], in_=below[:], compare_op=ALU.is_gt, fill=0.0, base=0,
                                  pattern=[[1, P]], channel_multiplier=-1))

            def split(k):
                _, _, src, hi, lo = all_pieces[k]
                pool.wait_ge(split_hi, k + 1)
                g.tensor_tensor(out=lo, in0=src, in1=hi.bitcast(F32), op=ALU.subtract).then_inc(split_lo, 1)

            def root(n, buf, width):
                pool.wait_ge(var_ready, n + 1)
                g.tensor_tensor(out=rstd[:, buf, 0:width], in0=mv[:, buf, 0:width, 1], in1=mhalf[:, 0:width],
                                op=ALU.pow).then_inc(rstd_ready, 1)

            pool.wait_ge(route1, 1)
            pool.wait_ge(d_init1, 16)
            done = 0
            for b in range(BATCH):
                root(LN1 + b, b % 2, 2)
                for i in range(2):
                    c = 2 * b + i
                    pool.wait_ge(row_ready, c + 1)
                    g.indirect_dma_start(out=scr1, out_offset=bass.IndirectOffsetOnAxis(ap=slot1[:, c:c + 1], axis=0),
                                         in_=ring[:, c % RING, :], in_offset=None, bounds_check=T * P - 1,
                                         oob_is_err=False).then_inc(d_scat[c % RING], 16)
                split(done)
                done += 1
            for _ in range(GAP_PIECES):
                split(done)
                done += 1
            pool.wait_ge(d_init2, 16)
            for i in range(T + 3):
                if 1 <= i <= T:
                    if i >= 3:
                        pool.wait_ge(x2_ready, i - 2)
                    root(LN2 + i - 1, (i - 1) % 2, 1)
                if 3 <= i:
                    t = i - 3
                    n = CHUNKS + t
                    pool.wait_ge(slot_ready, t + 1)
                    pool.wait_ge(x2_ready, t + 1)
                    g.indirect_dma_start(out=scr2, out_offset=bass.IndirectOffsetOnAxis(ap=slot2[:, t:t + 1], axis=0),
                                         in_=ring[:, n % RING, :], in_offset=None, bounds_check=E * REGION - 1,
                                         oob_is_err=False).then_inc(d_scat[n % RING], 16)
                if done < CTX_PIECES + Q_PIECES:
                    split(done)
                    done += 1
            assert done == CTX_PIECES + Q_PIECES
            for q in range(NQ):
                for t in range(T):
                    if q < NQ - 1:
                        for k in quarter_pieces(q + 1, t):
                            split(k)
            root(LN3, 0, 1)
            for t in range(T):
                n = CHUNKS + T + t
                if t + 1 < T:
                    root(LN3 + t + 1, (t + 1) % 2, 1)
                pool.wait_ge(out_ready, t + 1)
                g.indirect_dma_start(out=out, out_offset=bass.IndirectOffsetOnAxis(ap=outidx[:, t:t + 1], axis=0),
                                     in_=ring[:, n % RING, 0:D], in_offset=None, bounds_check=TOKENS - 1,
                                     oob_is_err=False).then_inc(d_scat[n % RING], 16)

        @block.tensor
        def _(pe):
            mm, tr = nc.tensor.matmul, nc.tensor.transpose

            def split_mm(dst, xhi, xlo, whi, wlo, start, stop):
                mm(dst, xhi, whi, start=start, stop=False)
                mm(dst, xhi, wlo, start=False, stop=False)
                return mm(dst, xlo, whi, start=False, stop=stop)

            def qk_of(b):
                if b >= 1:
                    pe.wait_ge(qk_copied, 2 * b)
                for k in range(DK):
                    last = mm(pQK[:, 0:SEQ], wqk[:, k, :], xT[:, k, b * SEQ:(b + 1) * SEQ],
                              start=k == 0, stop=k == DK - 1)
                last.then_inc(qk_done, 1)

            pe.wait_ge(d_aqk, 16)
            pe.wait_ge(d_xT0, 16)
            qk_of(0)
            pe.wait_ge(d_avo, 16)
            for d in range(DK):
                for k in range(DK):
                    last = mm(pW[:, d * D:(d + 1) * D], wv[:, k, d * P:(d + 1) * P], woT[:, k, :],
                              start=k == 0, stop=k == DK - 1)
            last.then_inc(wvo_done, 1)
            pe.wait_ge(consts, 14)
            pe.wait_ge(m1_ready, CHUNKS)
            R1 = pR1[:, 0:CHUNKS * E]
            mm(R1, below[:], m1[:].rearrange("p c e -> p (c e)"), start=True, stop=False)
            mm(R1, ones[:], m1cum[:, 0:CHUNKS, :].rearrange("p c e -> p (c e)"), start=False, stop=True)
            mm(pR1[:, 64:64 + E], ones[:], m1cum[:, CHUNKS, :], start=True, stop=True).then_inc(r1_done, 1)

            pe.wait_ge(d_wr, 32)
            for k in range(DK):
                mm(pWrSum, ones_f[:], wr[:, k, :], start=k == 0, stop=k == DK - 1)
            mm(pBr, one_row[:], br[:], start=True, stop=True).then_inc(br_done, 1)

            def ctx_router():
                pe.wait_ge(d_ctxn, 16)
                pe.wait_ge(wrc_ready, 1)
                for e in range(E):
                    for f in range(DK):
                        o = (e * DK + f) * E
                        for k in range(DK):
                            last = mm(pM[:, o:o + E], ctxn[:, e, k, f * P:(f + 1) * P], wrc[:, k, :],
                                      start=k == 0, stop=k == DK - 1)
                last.then_inc(m_done, 1)

            def z_of(b):
                pe.wait_ge(wvo_copied, 1)
                if b >= 1:
                    pe.wait_ge(z_copied, b)
                for i in range(2):
                    for k in range(DK):
                        o = b * SEQ + i * P
                        last = mm(pZ[:, i * D:(i + 1) * D], xT[:, k, o:o + P], wvo[:, k, :],
                                  start=k == 0, stop=k == DK - 1)
                last.then_inc(z_done, 1)

            def scores(b):
                pe.wait_ge(qk_copied, 2 * (b + 1))
                if b >= 2:
                    pe.wait_ge(exp_done, 2 * (b - 1))
                for i in range(2):
                    last = mm(pS[b % 2][:, i * SEQ:(i + 1) * SEQ], qk[:, b % 2, 0, i * P:(i + 1) * P],
                              qk[:, b % 2, 1, :], start=True, stop=True)
                last.then_inc(s_done, 1)

            def turn(b):
                pe.wait_ge(exp_done, 2 * (b + 1))
                if b >= 1:
                    pe.wait_ge(aT_copied, b)
                for j in range(2):
                    for i in range(2):
                        last = tr(pT[:, j * SEQ + i * P:j * SEQ + (i + 1) * P],
                                  at[:, b % 2, i, j * P:(j + 1) * P], ident[:])
                last.then_inc(t_done, 1)

            def mix(b):
                pe.wait_ge(aT_copied, b + 1)
                pe.wait_ge(z_copied, b + 1)
                pe.wait_ge(wrc_ready, 1)
                if b >= 1:
                    pe.wait_ge(o_read, 2 * b)
                for i in range(2):
                    for j in range(2):
                        last = mm(pO[:, i * D:(i + 1) * D], aT[:, b % 2, j, i * P:(i + 1) * P],
                                  zt[:, b % 2, j, :], start=j == 0, stop=j == 1)
                last.then_inc(o_done, 1)

            z_of(0)
            scores(0)
            pe.wait_ge(d_xT, 16)
            qk_of(1)
            z_of(1)
            scores(1)
            for b in range(BATCH):
                turn(b)
                if b + 2 < BATCH:
                    qk_of(b + 2)
                mix(b)
                if b + 2 < BATCH:
                    z_of(b + 2)
                    scores(b + 2)
            ctx_router()

            offs = {}

            def ctx_off(t):
                offs[t] = pe.value_load(off1[0:1, t:t + 1], min_val=0, max_val=(E - 1) * DK * CW)
                return offs[t]

            def tx(t):
                pe.wait_ge(d_rows[t], 16)
                if t >= 1:
                    pe.wait_ge(xlo_done, t)
                for k in range(DK):
                    last = tr(pX[:, k * P:(k + 1) * P], rows[:, t, k * P:(k + 1) * P], ident[:])
                last.then_inc(x_done, 1)

            def up(t):
                off = ctx_off(t)
                pe.wait_ge(xlo_done, t + 1)
                if t >= 1:
                    pe.wait_ge(h_done, t)
                for k in range(DK):
                    w = bass.ds(off + k * CW, E + D)
                    last = split_mm(pG[:, 0:E + D], x1T(t, 0)[:, k * P:(k + 1) * P], x1T(t, 1)[:, k * P:(k + 1) * P],
                                    ctx_hi[:, w], ctx_lo[:, w], k == 0, k == DK - 1)
                last.then_inc(g_done, 1)

            def th(t):
                pe.wait_ge(h_done, t + 1)
                if t >= 1:
                    pe.wait_ge(hlo_done, t)
                for k in range(DK):
                    last = tr(pH[:, k * P:(k + 1) * P], hid[:, t % 2, k * P:(k + 1) * P], ident[:])
                last.then_inc(ht_done, 1)

            def down(t):
                pe.wait_ge(hlo_done, t + 1)
                if t >= 1:
                    pe.wait_ge(y_read, t)
                off = offs.pop(t)
                for k in range(DK):
                    w = bass.ds(off + (k * CW + E), D + E)
                    last = split_mm(pY[:, 0:D + E], hT[:, t % 2, 0, k * P:(k + 1) * P], hT[:, t % 2, 1, k * P:(k + 1) * P],
                                    ctx_hi[:, w], ctx_lo[:, w], k == 0, k == DK - 1)
                last.then_inc(y_done, 1)

            def rank(t):
                pe.wait_ge(mask_ready, t + 1)
                if t >= 1:
                    pe.wait_ge(slot_ready, t)
                mm(pR[:, 0:E], below[:], m2[:, t, :], start=True, stop=False)
                mm(pR[:, 0:E], ones[:], m2cum[:, t, :], start=False, stop=True).then_inc(r_done, 1)

            pe.wait_ge(split_lo, CTX_PIECES)
            pe.wait_ge(router_lo, 2)
            pe.wait_ge(tables, 1)
            tx(0)
            for i in range(T + 3):
                for stage_of, t in ((up, i), (tx, i + 1), (down, i - 1), (rank, i - 3), (th, i)):
                    if 0 <= t < T and not (stage_of is tx and t == 0):
                        stage_of(t)
            mm(pL[:, 0:E], ones[:], m2cum[:, T, :], start=True, stop=True).then_inc(n_done, 1)

            def ftx(t):
                pe.wait_ge(d_rows[t], 32)
                if t >= 2:
                    pe.wait_ge(xlo_done, T + t - 1)
                for k in range(DK):
                    last = tr(fX[t % 2][:, k * P:(k + 1) * P], rows[:, t, k * P:(k + 1) * P], ident[:])
                last.then_inc(x_done, 1)

            def w_off(j):
                t = items[j][1]
                offs[j] = pe.value_load(off2[0:1, t:t + 1], min_val=0, max_val=(E - 1) * CHUNK)
                return offs[j]

            def fup(j):
                q, t = items[j]
                off = w_off(j)
                if t == 0:
                    pe.wait_ge(split_lo, CTX_PIECES + (q + 1) * Q_PIECES)
                if q == 0:
                    pe.wait_ge(xlo_done, T + t + 1)
                if j >= 2:
                    pe.wait_ge(h_done, T + j - 1)
                for k in range(DK):
                    w = bass.ds(off + ((q % 2) * E * CHUNK + k * 2 * FQ), 2 * FQ)
                    last = split_mm(fA[j % 2][:, :], x2s(t, 0)[:, k * P:(k + 1) * P], x2s(t, 1)[:, k * P:(k + 1) * P],
                                    w_hi[:, w], w_lo[:, w], k == 0, k == DK - 1)
                last.then_inc(g_done, 1)

            def fth(j):
                pe.wait_ge(h_done, T + j + 1)
                if j >= 2:
                    pe.wait_ge(hlo_done, T + j - 1)
                for k in range(FQ // P):
                    last = tr(fH[j % 2][:, k * P:(k + 1) * P], hid[:, (T + j) % 2, k * P:(k + 1) * P], ident[:])
                last.then_inc(ht_done, 1)

            def fdown(j):
                q, t = items[j]
                pe.wait_ge(hlo_done, T + j + 1)
                if j >= 2:
                    pe.wait_ge(y_read, T + j - 1)
                b = (T + j) % 2
                off = offs.pop(j)
                for k in range(FQ // P):
                    w = bass.ds(off + ((q % 2) * E * CHUNK + GU + k * D), D)
                    last = split_mm(fY[j % 2][:, 0:D], hT[:, b, 0, k * P:(k + 1) * P], hT[:, b, 1, k * P:(k + 1) * P],
                                    w_hi[:, w], w_lo[:, w], k == 0, k == FQ // P - 1)
                last.then_inc(y_done, 1)

            pe.wait_ge(tables, 2)
            ftx(0)
            for i in range(len(items) + 2):
                if i + 1 < T:
                    ftx(i + 1)
                if i < len(items):
                    fup(i)
                if 1 <= i <= len(items):
                    fth(i - 1)
                if i >= 2:
                    fdown(i - 2)

        @block.scalar
        def _(act):
            a = nc.scalar.activation
            act.dma_start(ids[:], ids_in).then_inc(d_ids, 16)
            act.dma_start(wr[:], wr_in.rearrange("p (k n) -> p k n", k=DK)).then_inc(d_wr, 16)
            act.dma_start(br[:], br_in).then_inc(d_wr, 16)

            def copy_qk(b):
                act.wait_ge(qk_done, b + 1)
                if b >= 2:
                    act.wait_ge(s_done, b - 1)
                for w in range(2):
                    a(qk[:, b % 2, w, :], pQK[w * RANK:(w + 1) * RANK, 0:SEQ], ACT.Copy).then_inc(qk_copied, 1)

            def copy_z(b):
                act.wait_ge(z_done, b + 1)
                if b >= 2:
                    act.wait_ge(o_done, b - 1)
                a(zt[:, b % 2, :, :].rearrange("p c d -> p (c d)"), pZ[:, :], ACT.Copy).then_inc(z_copied, 1)

            def exps(b):
                act.wait_ge(negmax_ready, b + 1)
                if b >= 2:
                    act.wait_ge(t_done, b - 1)
                for i in range(2):
                    a(at[:, b % 2, i, :], pS[b % 2][:, i * SEQ:(i + 1) * SEQ], ACT.Exp, bias=negmax[:, b % 2, i:i + 1],
                      accum_out=esum[:, b % 2, i:i + 1]).then_inc(exp_done, 1)

            def split(k):
                n, _, src, hi, _ = all_pieces[k]
                act.wait_ge(d_chunk[n % SLOTS], 16 * (n // SLOTS + 1))
                if n >= chunk_of(2, 0):
                    act.wait_ge(y_done, T + ((n - N_CTX) // E - 1) * T)
                a(hi, src, ACT.Copy).then_inc(split_hi, 1)

            act.wait_ge(consts, 14)
            a(gate[:, 0, 0:1], ones_f[:, 0:1], ACT.Exp)
            copy_qk(0)
            copy_z(0)
            copy_qk(1)
            exps(0)
            copy_z(1)
            done = 0
            for b in range(BATCH):
                act.wait_ge(t_done, b + 1)
                if b >= 2:
                    act.wait_ge(o_done, b - 1)
                a(aT[:, b % 2, :, :].rearrange("p j i -> p (j i)"), pT[:, :], ACT.Copy).then_inc(aT_copied, 1)
                if b + 1 < BATCH:
                    exps(b + 1)
                if b + 2 < BATCH:
                    copy_qk(b + 2)
                    copy_z(b + 2)
                split(done)
                done += 1
            a(gate[:, 0, 0:1], ones_f[:, 0:1], ACT.Silu)
            for _ in range(GAP_PIECES):
                split(done)
                done += 1
            act.wait_ge(wrc_ready, 1)
            for e in range(E):
                last = a(ctx_hi4[:, e, :, 0:E], wrc[:], ACT.Copy)
            last.then_inc(router_hi, 1)
            act.wait_ge(m_done, 1)
            a(ctx_hi4[:, :, :, E + D:CW], pM.rearrange("p (e k n) -> p e k n", e=E, k=DK),
              ACT.Copy).then_inc(router_hi, 1)

            def xhi(t):
                act.wait_ge(x_done, t + 1)
                if t >= 2:
                    act.wait_ge(g_done, t - 1)
                a(x1T(t, 0), pX[:, 0:D], ACT.Copy).then_inc(xhi_done, 1)

            def silu(t):
                act.wait_ge(g_done, t + 1)
                if t >= 2:
                    act.wait_ge(h_done, t - 1)
                a(gate[:, t % 2, :], pG[:, E:E + D], ACT.Silu).then_inc(silu_done, 1)

            def hhi(t):
                act.wait_ge(ht_done, t + 1)
                if t >= 2:
                    act.wait_ge(y_done, t - 1)
                a(hT[:, t % 2, 0, :], pH[:, 0:D], ACT.Copy).then_inc(hhi_done, 1)

            def norm_row(n, buf, row, done):
                act.wait_ge(nmr_ready, n + 1)
                a(row, row, ACT.Identity, bias=nmr[:, buf:buf + 1], scale=rstd[:, buf, 0:1]).then_inc(done, 1)

            def norm2(t):
                norm_row(t, t % 2, ring[:, (CHUNKS + t) % RING, 0:D], x2_ready)

            xhi(0)
            for i in range(T + 2):
                for stage_of, t in ((silu, i), (xhi, i + 1), (hhi, i), (norm2, i - 2)):
                    if 0 <= t < T and not (stage_of is xhi and t == 0):
                        stage_of(t)
                if done < CTX_PIECES + Q_PIECES:
                    split(done)
                    done += 1

            def fxhi(t):
                act.wait_ge(x_done, T + t + 1)
                if t == 0:
                    act.wait_ge(y_done, T)
                a(x2s(t, 0), fX[t % 2][:, 0:D], ACT.Copy).then_inc(xhi_done, 1)

            def fsilu(j):
                act.wait_ge(g_done, T + j + 1)
                act.wait_ge(h_done, T + j - 1)
                a(gate[:, (T + j) % 2, :], fA[j % 2][:, 0:FQ], ACT.Silu).then_inc(silu_done, 1)

            def fhhi(j):
                act.wait_ge(ht_done, T + j + 1)
                act.wait_ge(y_done, T + j - 1)
                a(hT[:, (T + j) % 2, 0, :], fH[j % 2][:, 0:FQ], ACT.Copy).then_inc(hhi_done, 1)

            fxhi(0)
            for i in range(len(items) + 4):
                if i + 1 < T:
                    fxhi(i + 1)
                if i < len(items):
                    fsilu(i)
                if 1 <= i <= len(items):
                    fhhi(i - 1)
                t = i - 4 - (len(items) - T)
                if t >= 0:
                    norm_row(T + t, t % 2, ring[:, (CHUNKS + T + t) % RING, 0:D], out_ready)
                if i < len(items):
                    q, t = items[i]
                    if q + 1 < NQ:
                        for k in quarter_pieces(q + 1, t):
                            split(k)
                if i == T:
                    a(lexp[:], rows[:, :, LOG:LOG + E], ACT.Exp).then_inc(lexp_done, 1)

        @block.vector
        def _(dve):
            v = nc.vector
            steps = [0]

            def step(ins):
                steps[0] += 1
                ins.then_inc(dve_step, 1)
                dve.wait_ge(dve_step, steps[0])

            def mark(ins):
                steps[0] += 1
                ins.then_inc(dve_step, 1)
                return steps[0]

            def after(n):
                dve.wait_ge(dve_step, n)

            def tile_tables(count_bank, col, fill):
                step(v.tensor_tensor(out=gt[:], in0=count_bank[:, col:col + E].unsqueeze(2).broadcast_to([P, E, CHUNKS]),
                                     in1=fill[:], op=ALU.is_gt))
                step(v.tensor_reduce(out=ntile[:], in_=gt[:], axis=AX.X, op=ALU.add))
                for e in range(1, E):
                    step(v.tensor_tensor(out=first[:, e:e + 1], in0=first[:, e - 1:e], in1=ntile[:, e - 1:e], op=ALU.add))
                step(v.tensor_tensor(out=past[:], in0=tile_no[:].unsqueeze(2).broadcast_to([P, T, E]),
                                     in1=first[:].unsqueeze(1).broadcast_to([P, T, E]), op=ALU.is_ge))
                step(v.tensor_reduce(out=expert[:], in_=past[:, :, 1:E], axis=AX.X, op=ALU.add))

            step(v.memset(first[:], 0.0))
            step(v.memset(m1cum[:], 0.0))
            step(v.memset(ge1[:], 0.0))
            step(v.memset(ge1[:, 0, :], 1.0))
            dve.wait_ge(d_ids, 16)
            step(v.tensor_copy(idf[:], ids[:]))
            for e in range(1, E):
                step(v.tensor_scalar(out=ge1[:, e, :], in0=idf[:], scalar1=float(e * PER_EXPERT), scalar2=None,
                                     op0=ALU.is_ge))
            step(v.tensor_tensor(out=m1[:].rearrange("p c e -> p e c"), in0=ge1[:, 0:E, :], in1=ge1[:, 1:E + 1, :],
                                 op=ALU.subtract))
            for c in range(CHUNKS):
                v.tensor_tensor(out=m1cum[:, c + 1, :], in0=m1cum[:, c, :], in1=m1[:, c, :],
                                op=ALU.add).then_inc(m1_ready, 1)
                dve.wait_ge(m1_ready, c + 1)
            dve.wait_ge(wvo_done, 1)
            v.tensor_copy(wvo.rearrange("p k n -> p (k n)"), pW[:, :]).then_inc(wvo_copied, 1)
            dve.wait_ge(br_done, 1)
            v.tensor_copy(br_all[:], pBr)
            v.scalar_tensor_tensor(out=wrc[:], in0=pWrSum.unsqueeze(1).broadcast_to([P, DK, E]), scalar=-1.0 / D,
                                   in1=wr[:], op0=ALU.mult, op1=ALU.add).then_inc(wrc_ready, 1)

            def maxes(b):
                dve.wait_ge(s_done, b + 1)
                step(v.reduce_max(negmax[:, b % 2, :], pS[b % 2][:, :].rearrange("p (i j) -> p i j", i=2), AX.X))
                v.tensor_scalar(out=negmax[:, b % 2, :], in0=negmax[:, b % 2, :], scalar1=-1.0, scalar2=None,
                                op0=ALU.mult).then_inc(negmax_ready, 1)

            maxes(0)
            maxes(1)
            dve.wait_ge(consts, 14)
            dve.wait_ge(r1_done, 1)
            tile_tables(pR1, 64, fill)
            v.tensor_scalar(out=off1[:], in0=expert[:], scalar1=float(DK * CW), scalar2=None,
                            op0=ALU.mult).then_inc(tables, 1)
            step(v.tensor_scalar(out=first128[:], in0=first[:], scalar1=float(P), scalar2=None, op0=ALU.mult))
            step(v.tensor_tensor(out=pos1[:], in0=pR1[:, 0:CHUNKS * E].rearrange("p (c e) -> p c e", e=E),
                                 in1=first128[:].unsqueeze(1).broadcast_to([P, CHUNKS, E]), op=ALU.add))
            step(v.tensor_tensor(out=pos1[:], in0=pos1[:], in1=m1[:], op=ALU.mult))
            step(v.tensor_reduce(out=slot1f[:], in_=pos1[:], axis=AX.X, op=ALU.add))
            v.tensor_copy(slot1[:], slot1f[:]).then_inc(route1, 1)
            v.tensor_scalar(out=m2cum[:, 0, :], in0=base2[:], scalar1=1.0 / P, scalar2=None, op0=ALU.mult)
            v.tensor_tensor(out=fill2[:], in0=fill[:], in1=base2[:].unsqueeze(2).broadcast_to([P, E, CHUNKS]),
                            op=ALU.add)
            def norm(n, buf, i, row, done):
                dve.wait_ge(rstd_ready, n + 1)
                v.tensor_scalar(out=row, in0=row, scalar1=mv[:, buf, i, 0:1], scalar2=rstd[:, buf, i:i + 1],
                                op0=ALU.subtract, op1=ALU.mult).then_inc(done, 1)

            def moments(buf, width, rowsof):
                for i in range(width):
                    step(v.bn_stats(stats[:, i, :], rowsof[i]))
                for i in range(width):
                    step(v.bn_aggr(mv[:, buf, i, :], stats[:, i, :]))
                v.tensor_scalar(out=mv[:, buf, 0:width, 1], in0=mv[:, buf, 0:width, 1], scalar1=EPS, scalar2=None,
                                op0=ALU.add).then_inc(var_ready, 1)

            dve.wait_ge(d_x, 16)
            for b in range(BATCH):
                dve.wait_ge(o_done, b + 1)
                step(v.reciprocal(rinv[:, b % 2, :], esum[:, b % 2, :]))
                for i in range(2):
                    c = 2 * b + i
                    if c >= RING:
                        dve.wait_ge(*scat(c - RING))
                    v.tensor_copy(ring[:, c % RING, TOK:TOK + 1], tok[:, c:c + 1])
                    v.memset(ring[:, c % RING, LOG:ROW], 0.0)
                    v.scalar_tensor_tensor(out=ring[:, c % RING, 0:D], in0=pO[:, i * D:(i + 1) * D],
                                           scalar=rinv[:, b % 2, i:i + 1], in1=xn[:, c, :],
                                           op0=ALU.mult, op1=ALU.add).then_inc(o_read, 1)
                dve.wait_ge(o_read, 2 * (b + 1))
                moments(b % 2, 2, [ring[:, (2 * b + i) % RING, 0:D] for i in range(2)])
                if b + 2 < BATCH:
                    maxes(b + 2)
                for i in range(2):
                    norm(LN1 + b, b % 2, i, ring[:, (2 * b + i) % RING, 0:D], row_ready)
            dve.wait_ge(router_hi, 2)
            v.tensor_tensor(out=ctx_lo4[:, :, :, 0:E], in0=wrc[:].unsqueeze(1).broadcast_to([P, E, DK, E]),
                            in1=ctx_hi4[:, :, :, 0:E].bitcast(F32), op=ALU.subtract).then_inc(router_lo, 1)
            v.tensor_tensor(out=ctx_lo4[:, :, :, E + D:CW], in0=pM.rearrange("p (e k n) -> p e k n", e=E, k=DK),
                            in1=ctx_hi4[:, :, :, E + D:CW].bitcast(F32), op=ALU.subtract).then_inc(router_lo, 1)

            def ring_of(t):
                return (CHUNKS + t) % RING

            def xlo(t):
                dve.wait_ge(xhi_done, t + 1)
                if t >= 2:
                    dve.wait_ge(g_done, t - 1)
                v.tensor_tensor(out=x1T(t, 1), in0=pX[:, 0:D], in1=x1T(t, 0).bitcast(F32),
                                op=ALU.subtract).then_inc(xlo_done, 1)

            def hidden(t):
                dve.wait_ge(silu_done, t + 1)
                if t >= 2:
                    dve.wait_ge(ht_done, t - 1)
                v.tensor_copy(x1logit[:, t % 2, :], pG[:, 0:E])
                v.tensor_tensor(out=hid[:, t % 2, :], in0=pG[:, E:E + D], in1=gate[:, t % 2, :],
                                op=ALU.mult).then_inc(h_done, 1)

            def hlo(t):
                dve.wait_ge(hhi_done, t + 1)
                v.tensor_tensor(out=hT[:, t % 2, 1, :], in0=pH[:, 0:D], in1=hT[:, t % 2, 0, :].bitcast(F32),
                                op=ALU.subtract).then_inc(hlo_done, 1)

            def validity():
                for t in range(T):
                    dve.wait_ge(d_rows[t], 16)
                step(v.tensor_scalar(out=valid[:], in0=rows[:, :, TOK], scalar1=float(TOKENS), scalar2=None,
                                     op0=ALU.is_lt))
                step(v.tensor_scalar(out=far[:], in0=valid[:], scalar1=-FAR, scalar2=FAR, op0=ALU.mult, op1=ALU.add))

            def in_phase2(t):
                return 0 <= t < T

            xlo(0)
            for i in range(T + 3):
                r, m, s = i - 1, i - 2, i - 3
                if i == 2:
                    validity()
                if in_phase2(i):
                    hidden(i)
                if in_phase2(m):
                    dve.wait_ge(rstd_ready, LN2 + m + 1)
                    dve.wait_ge(y_read, m + 1)
                    v.scalar_tensor_tensor(out=nmr[:, m % 2:m % 2 + 1], in0=mv[:, m % 2, 0, 0:1], scalar=-1.0,
                                           in1=rstd[:, m % 2, 0:1], op0=ALU.mult, op1=ALU.mult).then_inc(nmr_ready, 1)
                    m_logit = mark(v.scalar_tensor_tensor(out=logit[:], in0=rawlogit[:, m % 2, :],
                                                          scalar=rstd[:, m % 2, 0:1], in1=br_all[:],
                                                          op0=ALU.mult, op1=ALU.add))
                if in_phase2(i + 1):
                    xlo(i + 1)
                if in_phase2(m):
                    after(m_logit)
                    m_max = mark(v.reduce_max(lmax[:], logit[:], AX.X))
                row = ring[:, ring_of(r), 0:D]
                if in_phase2(r):
                    dve.wait_ge(y_done, r + 1)
                    dve.wait_ge(h_done, r + 1)
                    dve.wait_ge(*scat(CHUNKS + r - RING))
                    v.tensor_tensor(out=rawlogit[:, r % 2, :], in0=pY[:, D:D + E], in1=x1logit[:, r % 2, :], op=ALU.add)
                    v.tensor_tensor(out=row, in0=pY[:, 0:D], in1=rows[:, r, 0:D], op=ALU.add).then_inc(y_read, 1)
                lm = ring[:, ring_of(m), LOG:LOG + E]
                if in_phase2(m):
                    after(m_max)
                    m_rel = mark(v.tensor_scalar(out=lm, in0=logit[:], scalar1=lmax[:], scalar2=None,
                                                 op0=ALU.subtract))
                if in_phase2(s):
                    dve.wait_ge(r_done, s + 1)
                    s_own = mark(v.tensor_tensor(out=pos2[:], in0=pR[:, 0:E], in1=m2[:, s, :], op=ALU.mult))
                if in_phase2(i):
                    hlo(i)
                if in_phase2(m):
                    after(m_rel)
                    m_prio = mark(v.scalar_tensor_tensor(out=lw[:], in0=lm, scalar=0.0, in1=prio[:],
                                                         op0=ALU.is_ge, op1=ALU.mult))
                if in_phase2(s):
                    after(s_own)
                    s_sum = mark(v.reduce_sum(slot2f[:, s:s + 1], pos2[:], AX.X))
                if in_phase2(r):
                    v.tensor_copy(ring[:, ring_of(r), TOK:TOK + 1], rows[:, r, TOK:TOK + 1])
                    dve.wait_ge(y_read, r + 1)
                    r_stats = mark(v.bn_stats(stats[:, 0, :], row))
                if in_phase2(m):
                    after(m_prio)
                    m_top = mark(v.reduce_max(lwmax[:], lw[:], AX.X))
                if in_phase2(s):
                    after(s_sum)
                    v.tensor_scalar(out=slot2[:, s:s + 1], in0=slot2f[:, s:s + 1], scalar1=far[:, s:s + 1],
                                    scalar2=None, op0=ALU.add).then_inc(slot_ready, 1)
                if in_phase2(r):
                    after(r_stats)
                    r_mv = mark(v.bn_aggr(mv[:, r % 2, 0, :], stats[:, 0, :]))
                if in_phase2(m):
                    after(m_top)
                    m_one = mark(v.tensor_scalar(out=m2[:, m, :], in0=lw[:], scalar1=lwmax[:],
                                                 scalar2=valid[:, m:m + 1], op0=ALU.is_equal, op1=ALU.mult))
                if in_phase2(r):
                    after(r_mv)
                    v.tensor_scalar(out=mv[:, r % 2, 0:1, 1], in0=mv[:, r % 2, 0:1, 1], scalar1=EPS, scalar2=None,
                                    op0=ALU.add).then_inc(var_ready, 1)
                if in_phase2(m):
                    after(m_one)
                    if m >= 1:
                        dve.wait_ge(mask_ready, m)
                    v.tensor_tensor(out=m2cum[:, m + 1, :], in0=m2cum[:, m, :], in1=m2[:, m, :],
                                    op=ALU.add).then_inc(mask_ready, 1)

            dve.wait_ge(n_done, 1)
            tile_tables(pL, 0, fill2)
            step(v.tensor_scalar(out=off2[:], in0=expert[:], scalar1=float(CHUNK), scalar2=None, op0=ALU.mult))
            step(v.tensor_tensor(out=pastf[:], in0=past[:], in1=first[:].unsqueeze(1).broadcast_to([P, T, E]), op=ALU.mult))
            step(v.reduce_max(begun[:], pastf[:], AX.X))
            step(v.tensor_tensor(out=begun[:], in0=tile_no[:], in1=begun[:], op=ALU.subtract))
            step(v.scalar_tensor_tensor(out=blk[:], in0=expert[:], scalar=float(REGION // P), in1=begun[:],
                                        op0=ALU.mult, op1=ALU.add))
            v.tensor_scalar(out=row2[:], in0=blk[:], scalar1=float(P), scalar2=None, op0=ALU.mult).then_inc(tables, 1)

            def fxlo(t):
                dve.wait_ge(xhi_done, T + t + 1)
                v.tensor_tensor(out=x2s(t, 1), in0=fX[t % 2][:, 0:D], in1=x2s(t, 0).bitcast(F32),
                                op=ALU.subtract).then_inc(xlo_done, 1)

            def fhidden(j):
                dve.wait_ge(silu_done, T + j + 1)
                dve.wait_ge(ht_done, T + j - 1)
                v.tensor_tensor(out=hid[:, (T + j) % 2, :], in0=fA[j % 2][:, FQ:2 * FQ], in1=gate[:, (T + j) % 2, :],
                                op=ALU.mult).then_inc(h_done, 1)

            def fhlo(j):
                dve.wait_ge(hhi_done, T + j + 1)
                v.tensor_tensor(out=hT[:, (T + j) % 2, 1, :], in0=fH[j % 2][:, 0:FQ],
                                in1=hT[:, (T + j) % 2, 0, :].bitcast(F32), op=ALU.subtract).then_inc(hlo_done, 1)

            def fsum(j):
                q, t = items[j]
                dve.wait_ge(y_done, T + j + 1)
                if q == 0:
                    v.tensor_copy(acc[:, t, :], fY[j % 2][:, 0:D]).then_inc(y_read, 1)
                elif q < NQ - 1:
                    v.tensor_tensor(out=acc[:, t, :], in0=fY[j % 2][:, 0:D], in1=acc[:, t, :],
                                    op=ALU.add).then_inc(y_read, 1)
                if q == NQ - 2:
                    dve.wait_ge(y_read, T + j + 1)
                    step(v.scalar_tensor_tensor(out=acc[:, t, :], in0=acc[:, t, :], scalar=topw[:, t:t + 1],
                                                in1=rows[:, t, 0:D], op0=ALU.mult, op1=ALU.add))

            def gates():
                dve.wait_ge(lexp_done, 1)
                step(v.reduce_sum(lsum[:], lexp[:], AX.X))
                step(v.reciprocal(topw[:], lsum[:]))
                step(v.tensor_copy(outidx[:], rows[:, :, TOK]))

            def finish(t):
                n = CHUNKS + T + t
                dve.wait_ge(*scat(n - RING))
                dve.wait_ge(y_done, T + len(items) - T + t + 1)
                r = ring[:, n % RING, 0:D]
                v.scalar_tensor_tensor(out=r, in0=fY[(len(items) - T + t) % 2][:, 0:D], scalar=topw[:, t:t + 1],
                                       in1=acc[:, t, :], op0=ALU.mult, op1=ALU.add).then_inc(y_read, 1)
                dve.wait_ge(y_read, len(items) + t + 1)
                moments(t % 2, 1, [r])

            def finish_norm(t):
                dve.wait_ge(rstd_ready, LN3 + t + 1)
                if t >= 2:
                    dve.wait_ge(out_ready, t - 1)
                v.scalar_tensor_tensor(out=nmr[:, t % 2:t % 2 + 1], in0=mv[:, t % 2, 0, 0:1], scalar=-1.0,
                                       in1=rstd[:, t % 2, 0:1], op0=ALU.mult, op1=ALU.mult).then_inc(nmr_ready, 1)

            fxlo(0)
            for i in range(len(items) + 3):
                if i + 1 < T:
                    fxlo(i + 1)
                if i < len(items):
                    fhidden(i)
                if 1 <= i <= len(items):
                    fhlo(i - 1)
                if 2 <= i <= len(items) + 1 - T:
                    fsum(i - 2)
                if i == T + 1:
                    gates()
                if i - 2 >= 3 * T and i - 2 < len(items):
                    finish(i - 2 - 3 * T)
                if i - 3 >= 3 * T:
                    finish_norm(i - 3 - 3 * T)


def kernel(**inputs):
    import concourse.bacc as bacc
    from concourse.bass_utils import run_bass_kernel_spmd

    def rows_first(a, k):
        n = a.shape[-1]
        return np.ascontiguousarray(a.reshape(k, P, n).transpose(1, 0, 2).reshape(P, k * n))

    x = np.asarray(inputs["x"]).reshape(TOKENS, D)
    wq, wk = np.asarray(inputs["L0_attn_Wq"]), np.asarray(inputs["L0_attn_Wk"])
    wv, wo = np.asarray(inputs["L0_attn_Wv"]), np.asarray(inputs["L0_attn_Wo"])
    ctx = np.asarray(inputs["ctx_2048"])
    wg, wu, wd = (np.asarray(inputs[f"L0_ffn_W{c}"]) for c in "gud")
    aw = np.concatenate([rows_first(np.concatenate([wq, wk], 0).T, DK), rows_first(wv, DK), rows_first(wo.T, DK)], 1)
    ctxT = np.concatenate([rows_first(ctx[e].T, DK) for e in range(E)], 1)
    chunks = []
    for q in range(NQ):
        f = slice(q * FQ, (q + 1) * FQ)
        for e in range(E):
            gu = rows_first(np.concatenate([wg[e][:, f], wu[e][:, f]], 1), DK)
            chunks.append(np.concatenate([gu, rows_first(wd[e][f, :], FQ // P)], 1))
    arrays = {
        "in_attn_w": np.ascontiguousarray(aw),
        "in_xT": rows_first(x.T, DK),
        "in_x_tok": rows_first(x, CHUNKS),
        "in_ids": np.ascontiguousarray(np.asarray(inputs["itok_BxS_13_99985"]).reshape(CHUNKS, P).T),
        "in_wr": rows_first(np.asarray(inputs["L0_ffn_Wr"]), DK),
        "in_br": np.ascontiguousarray(np.asarray(inputs["L0_ffn_br"]).reshape(1, E)),
        "in_ctxT": np.ascontiguousarray(ctxT),
        "in_ctx": np.concatenate([rows_first(ctx[e], DK) for e in range(E)], 1),
        "in_w_ffn": np.ascontiguousarray(np.stack(chunks)),
    }
    nc = bacc.Bacc("TRN2", target_bir_lowering=False, num_devices=1)
    args = [nc.dram_tensor(n, a.shape, mybir.dt.from_np(a.dtype), kind="ExternalInput").ap() for n, a in arrays.items()]
    out = nc.dram_tensor("out_tokens", (TOKENS, D), F32, kind="ExternalOutput").ap()
    route_kernel(nc, *args, out)
    got = run_bass_kernel_spmd(nc, [arrays], core_ids=[0]).results[0]["out_tokens"]
    return got.reshape(BATCH, SEQ, D)
```
